# Optimizing a Trainium2 kernel written in Bass

```python
import numpy as np
import jax
import jax.numpy as jnp

def _softmax(x, axis=-1):
    return jax.nn.softmax(x, axis=axis)

def _gelu(x):
    return jax.nn.gelu(x, approximate=True)

def _silu(x):
    return jax.nn.silu(x)

def _sigmoid(x):
    return jax.nn.sigmoid(x)

def _layernorm(x, axis=-1, eps=1e-05):
    m = jnp.mean(x, axis=axis, keepdims=True)
    v = jnp.var(x, axis=axis, keepdims=True)
    return (x - m) / jnp.sqrt(v + eps)

def _scatter_add(tgt, idx, src, axis=0):
    return tgt.at[idx].add(src)

def _segment_sum(src, seg, n):
    return jax.ops.segment_sum(src, seg, n)
kernel_name = 'mk_gnn_preln_d1_gnn_r8_573406'

def setup_inputs(seed: int=0):
    np.random.seed(seed)
    _w = jnp.asarray

    def _rec_inputs():
        import jax
        import jax.numpy as jnp
        _gk = jax.random.key(seed)
        x = -0.000202 + 1 * jax.random.normal(jax.random.fold_in(_gk, 1), (6250, 128), jnp.float32)
        src = jax.random.randint(jax.random.fold_in(_gk, 2), (200000,), 0, 6250, jnp.int32)
        dst = jnp.minimum((6250 * jax.random.uniform(jax.random.fold_in(_gk, 3), (200000,)) ** 2.0).astype(jnp.int32), 49999)
        _o = jnp.argsort(dst, stable=True)
        src = src[_o]
        dst = dst[_o]
        edge_attr_128 = -5.16925e-05 + 1.00005 * jax.random.normal(jax.random.fold_in(_gk, 12), (200000, 128), jnp.float32)
        return (x, src, dst, edge_attr_128)
    x, src, dst, edge_attr_128 = _rec_inputs()

    def _L0_gnn_setup():
        import jax, jax.numpy as jnp
        import numpy as np
        C = 128
        N_NODES = 6250
        N_EDGES = 100000
        BN_EPS = 1e-05

        def batchnorm(h, w, b):
            mu = jnp.mean(h, axis=0)
            var = jnp.mean((h - mu) ** 2, axis=0)
            return (h - mu) * jax.lax.rsqrt(var + BN_EPS) * w + b
        key = jax.random.key(seed)
        ks = jax.random.split(key, 10)
        lim1 = 1.0 / np.sqrt(2 * C)
        lim2 = 1.0 / np.sqrt(2 * C)
        return {'x': jax.random.normal(ks[0], (N_NODES, C), dtype=jnp.float32), 'edge_index': jax.random.randint(ks[1], (2, N_EDGES), 0, N_NODES), 'edge_attr': jax.random.normal(ks[2], (N_EDGES, C), dtype=jnp.float32), 'u': jax.random.normal(ks[3], (256, C), dtype=jnp.float32), 'batch': jax.random.randint(ks[4], (N_NODES,), 0, 256), 'w1': jax.random.uniform(ks[5], (C, 2 * C), jnp.float32, -lim1, lim1), 'b1': jax.random.uniform(ks[6], (C,), jnp.float32, -lim1, lim1), 'bn1_w': jnp.ones((C,), jnp.float32), 'bn1_b': jnp.zeros((C,), jnp.float32), 'w2': jax.random.uniform(ks[7], (C, 2 * C), jnp.float32, -lim2, lim2), 'b2': jax.random.uniform(ks[8], (C,), jnp.float32, -lim2, lim2), 'bn2_w': jnp.ones((C,), jnp.float32), 'bn2_b': jnp.zeros((C,), jnp.float32)}
    _L0_gnn_all = _L0_gnn_setup()
    _L0_gnn_in = {k: v for k, v in _L0_gnn_all.items() if k in ('u', 'w1', 'b1', 'bn1_w', 'bn1_b', 'w2', 'b2', 'bn2_w', 'bn2_b')}
    del _L0_gnn_all
    return {'x': x, 'src': src, 'dst': dst, 'edge_attr_128': edge_attr_128, 'L0_gnn_u': _L0_gnn_in['u'], 'L0_gnn_w1': _L0_gnn_in['w1'], 'L0_gnn_b1': _L0_gnn_in['b1'], 'L0_gnn_bn1_w': _L0_gnn_in['bn1_w'], 'L0_gnn_bn1_b': _L0_gnn_in['bn1_b'], 'L0_gnn_w2': _L0_gnn_in['w2'], 'L0_gnn_b2': _L0_gnn_in['b2'], 'L0_gnn_bn2_w': _L0_gnn_in['bn2_w'], 'L0_gnn_bn2_b': _L0_gnn_in['bn2_b']}

def reference(x, src, dst, edge_attr_128, L0_gnn_u, L0_gnn_w1, L0_gnn_b1, L0_gnn_bn1_w, L0_gnn_bn1_b, L0_gnn_w2, L0_gnn_b2, L0_gnn_bn2_w, L0_gnn_bn2_b):
    import jax
    import jax.numpy as jnp

    def _L0_gnn_ref(x, edge_index, edge_attr, u, batch, w1, b1, bn1_w, bn1_b, w2, b2, bn2_w, bn2_b):
        import jax, jax.numpy as jnp
        import numpy as np
        C = 128
        N_NODES = 6250
        N_EDGES = 100000
        BN_EPS = 1e-05

        def batchnorm(h, w, b):
            mu = jnp.mean(h, axis=0)
            var = jnp.mean((h - mu) ** 2, axis=0)
            return (h - mu) * jax.lax.rsqrt(var + BN_EPS) * w + b
        row, col = (edge_index[0], edge_index[1])
        n = x.shape[0]
        h = jnp.concatenate([x[row], edge_attr], axis=1)
        h = h @ w1.T + b1
        h = jax.nn.elu(batchnorm(h, bn1_w, bn1_b))
        s = jax.ops.segment_sum(h, col, num_segments=n)
        cnt = jax.ops.segment_sum(jnp.ones((h.shape[0],), h.dtype), col, num_segments=n)
        agg = s / jnp.maximum(cnt, 1.0)[:, None]
        out = jnp.concatenate([x, agg], axis=1) @ w2.T + b2
        return jax.nn.elu(batchnorm(out, bn2_w, bn2_b))
    edge_index = jnp.stack([src, dst])
    batch0 = jnp.zeros((6250,), jnp.int32)
    h = jnp.maximum(_layernorm(x, axis=-1), 0.0)
    x = x + _L0_gnn_ref(h, edge_index, edge_attr_128, L0_gnn_u, batch0, L0_gnn_w1, L0_gnn_b1, L0_gnn_bn1_w, L0_gnn_bn1_b, L0_gnn_w2, L0_gnn_b2, L0_gnn_bn2_w, L0_gnn_bn2_b)
    return x

_drawn_inputs = setup_inputs


def setup_inputs(seed=0):
    import zlib

    import numpy as np

    out = dict(_drawn_inputs(seed))
    spreads = {'L0_gnn_bn1_w': (1.0, 0.586),
     'L0_gnn_bn1_b': (0.0, 0.8),
     'L0_gnn_bn2_w': (1.0, 0.2),
     'L0_gnn_bn2_b': (0.0, 0.1)}
    factors = {'L0_gnn_b1': 8.0, 'L0_gnn_b2': 8.0}
    for name, (base, spread) in spreads.items():
        noise = np.random.default_rng([zlib.crc32(name.encode()), seed]).standard_normal(out[name].shape)
        drawn = base * np.exp(spread * noise) if base else spread * noise
        out[name] = jnp.asarray(drawn.astype(out[name].dtype))
    for name, factor in factors.items():
        out[name] = (out[name] * factor).astype(out[name].dtype)
    return out
```

```python
from contextlib import ExitStack

import concourse.bass as bass
from concourse import mybir

F32 = mybir.dt.float32
BF16 = mybir.dt.bfloat16
I32 = mybir.dt.int32
U32 = mybir.dt.uint32
ALU = mybir.AluOpType
ACT = mybir.ActivationFunctionType
AX_X = mybir.AxisListType.X
ds = bass.ds

P = 128
K = 4
GE = P * K
U = 6
H = U // 2
NPS = 3
WIN = 64
BANK = 512
LN_EPS = 1e-5
BN_EPS = 1e-5
LT = 7


def wait(eng, sem, value):
    if isinstance(value, int) and value <= 0:
        return
    eng.wait_ge(sem, value)


def norm(it, s, unroll):
    return it + s // unroll, s % unroll


def exists(it):
    return not (isinstance(it, int) and it < 0)


def gnn_kernel(nc, x, src, dst, edge_attr, w1, b1, bn1_w, bn1_b, w2, b2, bn2_w, bn2_b, out):
    N, C = x.shape
    E = edge_attr.shape[0]
    assert C == P
    NT = -(-N // P)
    NP = NT * P
    N_LAST = N - (NT - 1) * P
    LTURNS = NT // LT
    assert LTURNS * LT == NT
    FULL = E // GE
    TURNS = FULL // U
    assert TURNS * U == FULL and TURNS >= 3
    TAIL_ROWS = (E - FULL * GE) // K
    assert 0 < TAIL_ROWS < P and FULL * GE + TAIL_ROWS * K == E
    GROUPS = FULL + 1
    BLK = -(-GROUPS // P)
    B_ROWS = FULL - (BLK - 1) * P
    TAIL_E = TAIL_ROWS * K
    SWIN = BANK
    NWIN = -(-N // SWIN)
    TABLE = max(NWIN * SWIN, N + WIN)
    CH = BANK
    CHF = N // CH
    U3 = 2
    TURNS3 = CHF // U3
    assert TURNS3 * U3 == CHF and TURNS3 >= 3
    CH_TAIL = N - CHF * CH
    assert CH_TAIL <= P

    p_dram = nc.dram_tensor("p_table", [NP, C], F32, kind="Internal").ap()
    z_dram = nc.dram_tensor("z_edges", [2 * TURNS + 1, P, H * GE], F32, kind="Internal").ap()
    base_dram = nc.dram_tensor("base_row_dram", [BLK * P], I32, kind="Internal").ap()

    with ExitStack() as ctx:
        def sb(name, shape, dt=F32):
            return ctx.enter_context(nc.sbuf_tensor(name, shape, dt))

        def sem(name):
            return ctx.enter_context(nc.semaphore(name))

        ps = ctx.enter_context(nc.psum_tensor("ps", [P, 8, BANK], F32))

        ident = sb("ident", [P, P])
        ones_bf = sb("ones_bf", [P, P], BF16)
        minus_half = sb("minus_half", [P, LT])
        minus_one = sb("minus_one", [P, LT])
        ln_eps = sb("ln_eps", [P, LT])
        iota = sb("iota", [P, SWIN])
        w1_sb = sb("w1_sb", [P, 2 * C])
        w2_sb = sb("w2_sb", [P, 2 * C])
        wT = sb("wT", [P, 4, C])
        b1_rows = sb("b1_rows", [P, C])
        vecs = sb("vecs", [P, 5])
        x_sb = sb("x_sb", [P, NT, C])
        hT = sb("hT", [P, NP])
        agg = sb("agg", [P, 2, TABLE])
        agg_flat = agg[:, :, :].rearrange("p a n -> p (a n)")
        src_idx = sb("src_idx", [P, BLK * P, K], I32)
        rel_dst = sb("rel_dst", [P, BLK * P, K])
        abs_dst = sb("abs_dst", [P, BLK * P, K])
        base_row = sb("base_row", [1, BLK * P], I32)
        flag = sb("flag", [1, 1], I32)
        IB = BLK * GE
        assert 5 * IB <= 2 * TABLE
        raw = [agg_flat[:, i * IB:(i + 1) * IB] for i in range(5)]
        src_raw = raw[0].bitcast(I32).rearrange("p (j e) -> p j e", j=BLK)
        dst_raw = raw[1].bitcast(I32).rearrange("p (j e) -> p j e", j=BLK)
        src_f, dst_f, rel_f = [r.rearrange("p (j e) -> p j e", j=BLK) for r in raw[2:5]]
        dmin = sb("dmin", [P, BLK])
        dmax = sb("dmax", [P, BLK])
        dspan = sb("dspan", [P, BLK])
        dspan1 = sb("dspan1", [P, 1])
        span_all = sb("span_all", [1, 1])
        base_i = sb("base_i", [P, BLK], I32)
        ln_st = sb("ln_st", [P, LT, 6])
        ln_mv = sb("ln_mv", [P, LT, 2])
        rstd = sb("rstd", [P, LT])
        ln_bias = sb("ln_bias", [P, LT])
        e_buf = sb("e_buf", [P, U, GE])
        z_buf = sb("z_buf", [P, U, GE])
        g_buf = sb("g_buf", [P, U, GE])
        t_buf = sb("t_buf", [P, NPS, GE])
        idx_now = sb("idx_now", [P, U, K], I32)
        one_hot = sb("one_hot", [P, NPS, K, WIN])
        win_sum = sb("win_sum", [P, 2, 2, WIN])
        stats = sb("stats", [P, GROUPS, 6])
        bn_mv = sb("bn_mv", [P, 2])
        bn_k = sb("bn_k", [P, 5])
        stats2 = sb("stats2", [P, CHF + 1, 6])
        bn2_mv = sb("bn2_mv", [P, 2])
        bn2_k = sb("bn2_k", [P, 5])
        h_st = e_buf[:, 0:2, :].rearrange("p a b -> p (a b)")[:, 0:LT * P]
        hT_st = e_buf[:, 2:4, :].rearrange("p a b -> p (a b)")[:, 0:LT * P]
        p_st = e_buf[:, 4:6, :].rearrange("p a b -> p (a b)")[:, 0:LT * P]

        x_cleared = sem("x_cleared")
        x_in = sem("x_in")
        w_in = sem("w_in")
        vec_in = sem("vec_in")
        idx_cleared = sem("idx_cleared")
        src_in = sem("src_in")
        dst_in = sem("dst_in")
        ident_zero = sem("ident_zero")
        consts_ready = sem("consts_ready")
        w_turned = sem("w_turned")
        wT_ready = sem("wT_ready")
        idx_float = sem("idx_float")
        dminmax = sem("dminmax")
        rel_ready = sem("rel_ready")
        base_ready = sem("base_ready")
        base_out = sem("base_out")
        base_in = sem("base_in")
        span_step = sem("span_step")
        span_turned = sem("span_turned")
        flag_ready = sem("flag_ready")
        idx_turned = sem("idx_turned")
        idx_kept = sem("idx_kept")
        table_cleared = sem("table_cleared")
        ln_step = sem("ln_step")
        ln_root = sem("ln_root")
        ln_ready = sem("ln_ready")
        h_ready = sem("h_ready")
        h_turned = sem("h_turned")
        hT_copied = sem("hT_copied")
        hT_saved = sem("hT_saved")
        p_product = sem("p_product")
        p_added = sem("p_added")
        p_out = sem("p_out")
        e_in = [sem(f"e_in{h}") for h in range(2)]
        z_out = [sem(f"z_out{h}") for h in range(2)]
        g_in = [sem(f"g_in{s}") for s in range(U)]
        idx_copied = sem("idx_copied")
        e_turned = sem("e_turned")
        eT_ready = sem("eT_ready")
        z_ready = sem("z_ready")
        z_counted = sem("z_counted")
        z_saved = sem("z_saved")
        bn_step = sem("bn_step")
        bn_root = sem("bn_root")
        bn1_ready = sem("bn1_ready")
        z_in = [sem(f"z_in{h}") for h in range(2)]
        exp_ready = sem("exp_ready")
        lin_ready = sem("lin_ready")
        elu_ready = sem("elu_ready")
        elu_turned = sem("elu_turned")
        elu_edges = sem("elu_edges")
        hot_ready = sem("hot_ready")
        win_ready = sem("win_ready")
        win_copied = sem("win_copied")
        win_added = sem("win_added")
        slow_in = sem("slow_in")
        slow_exp = sem("slow_exp")
        slow_lin = sem("slow_lin")
        slow_elu = sem("slow_elu")
        slow_turned = sem("slow_turned")
        slow_edges = sem("slow_edges")
        slow_dst = sem("slow_dst")
        slow_hot = sem("slow_hot")
        slow_win = sem("slow_win")
        slow_added = sem("slow_added")
        agg_done = sem("agg_done")
        mean_step = sem("mean_step")
        mean_ready = sem("mean_ready")
        y_ready = sem("y_ready")
        y_kept = sem("y_kept")
        y_counted = sem("y_counted")
        bn2_ready = sem("bn2_ready")
        yexp_ready = sem("yexp_ready")
        ylin_ready = sem("ylin_ready")
        yelu_ready = sem("yelu_ready")
        yelu_turned = sem("yelu_turned")
        res_ready = sem("res_ready")
        res_out = [sem(f"res_out{s}") for s in range(U3)]

        e_full = edge_attr[0:FULL * GE, :].rearrange("(g p k) c -> p g (k c)", p=P, k=K)
        e_tail = edge_attr[FULL * GE:E, :].rearrange("(p k) c -> p (k c)", k=K)
        out_full = out[0:CHF * CH, :].rearrange("(n t p) c -> p n t c", p=P, t=CH // P)

        def count(it, s):
            return it * U + s

        edge_bank = [ps[:, b, :] for b in range(NPS)]
        z_bank = [ps[:, NPS + b, :] for b in range(NPS)]
        win_bank = [ps[:, 6 + b, :] for b in range(2)]

        def edge_turns(eng, turn):
            turn(0)
            with eng.Fori(1, TURNS - 1) as it:
                turn(it)
            turn(TURNS - 1)

        def node_turns(eng, turn, first=0, last=LTURNS):
            turn(first)
            with eng.Fori(first + 1, last) as it:
                turn(it)

        block = ctx.enter_context(nc.Block())

        @block.sync
        def _(sp):
            sp.dma_start(w1_sb[:, :], w1).then_inc(w_in, 16)
            sp.dma_start(w2_sb[:, :], w2).then_inc(w_in, 16)
            last_x = NT - 1
            sp.dma_start(x_sb[:, 0:last_x, :], x[0:last_x * P, :].rearrange("(t p) c -> p t c", p=P)).then_inc(x_in, 16)
            sp.wait_ge(x_cleared, 1)
            sp.dma_start(x_sb[0:N_LAST, last_x, :], x[last_x * P:N, :]).then_inc(x_in, 16)
            sp.wait_ge(idx_cleared, 2)
            b0 = (BLK - 1) * P * GE
            for raw_idx, ids, landed in ((dst_raw, dst, dst_in), (src_raw, src, src_in)):
                sp.dma_start(raw_idx[:, 0:BLK - 1, :], ids[0:b0].rearrange("(j g e) -> g j e", g=P, e=GE)).then_inc(landed, 16)
                sp.dma_start(raw_idx[0:B_ROWS, BLK - 1, :], ids[b0:FULL * GE].rearrange("(g e) -> g e", e=GE)).then_inc(landed, 16)
                sp.dma_start(raw_idx[B_ROWS:B_ROWS + 1, BLK - 1, 0:TAIL_E],
                             ids[FULL * GE:E].rearrange("(g e) -> g e", g=1)).then_inc(landed, 16)
                sp.dma_start(raw_idx[B_ROWS:B_ROWS + 1, BLK - 1, TAIL_E:GE],
                             ids[FULL * GE:FULL * GE + GE - TAIL_E].rearrange("(g e) -> g e", g=1)).then_inc(landed, 16)
            sp.dma_start(b1_rows[:, :], b1.partition_broadcast(P)).then_inc(vec_in, 16)
            for i, v in enumerate((bn1_w, bn1_b, b2, bn2_w, bn2_b)):
                sp.dma_start(vecs[:, i:i + 1], v.rearrange("(c o) -> c o", o=1)).then_inc(vec_in, 16)
            sp.wait_ge(base_ready, 1)
            sp.dma_start(base_dram.rearrange("(j g) -> g j", g=P), base_i[:, :], allow_slow_non_contiguous=True).then_inc(base_out, 16)
            sp.wait_ge(base_out, 16)
            sp.dma_start(base_row[:, :], base_dram.rearrange("(o g) -> o g", o=1)).then_inc(base_in, 16)
            p_view = p_dram.rearrange("(n t p) c -> p n t c", p=P, t=LT)
            def turn_a(it):
                sp.wait_ge(p_added, it + 1)
                sp.dma_start(p_view[:, ds(it, 1), :, :].rearrange("p n t c -> p (n t) c"),
                             p_st.rearrange("p (t c) -> p t c", c=C)).then_inc(p_out, 16)
            node_turns(sp, turn_a)
            sp.wait_ge(p_out, 16 * LTURNS)
            sp.wait_ge(hT_saved, LTURNS)

            def load_edges(it, h):
                wait(sp, e_turned, count(it - 1, h * H + H))
                sp.dma_start(e_buf[:, h * H:(h + 1) * H, :], e_full[:, ds(count(it, h * H), H), :]).then_inc(e_in[h], 16)

            def store_z(it, h):
                wait(sp, z_saved, count(it, h * H + H))
                sp.dma_start(z_dram[ds(2 * it + h, 1), :, :].rearrange("n p f -> (n p) f"),
                             z_buf[:, h * H:(h + 1) * H, :].rearrange("p a b -> p (a b)")).then_inc(z_out[h], 16)

            def turn_b(it):
                for h in range(2):
                    load_edges(it, h)
                    if exists(it - 1):
                        store_z(it - 1, h)

            edge_turns(sp, turn_b)
            sp.wait_ge(e_turned, count(TURNS - 1, H))
            sp.dma_start(e_buf[0:TAIL_ROWS, 0, :], e_tail).then_inc(e_in[0], 16)
            for h in range(2):
                store_z(TURNS - 1, h)
            sp.wait_ge(z_saved, GROUPS)
            sp.dma_start(z_dram[2 * TURNS, :, 0:TAIL_E], z_buf[:, 0, 0:TAIL_E]).then_inc(z_out[0], 16)
            sp.wait_ge(z_out[0], 16 * (TURNS + 1))
            sp.wait_ge(z_out[1], 16 * TURNS)
            sp.wait_ge(e_turned, GROUPS)

            def load_z(it, h):
                wait(sp, elu_ready, count(it - 1, h * H + H))
                sp.dma_start(e_buf[:, h * H:(h + 1) * H, :].rearrange("p a b -> p (a b)"),
                             z_dram[ds(2 * it + h, 1), :, :].rearrange("n p f -> (n p) f")).then_inc(z_in[h], 16)

            def turn_c(it):
                for h in range(2):
                    load_z(it, h)

            sp.wait_ge(flag_ready, 1)
            wide = sp.value_load(flag[0:1, 0:1], min_val=0, max_val=N)
            with sp.If(wide < WIN):
                edge_turns(sp, turn_c)
                sp.wait_ge(elu_ready, count(TURNS - 1, H))
                sp.dma_start(e_buf[:, 0, 0:TAIL_E], z_dram[2 * TURNS, :, 0:TAIL_E]).then_inc(z_in[0], 16)
            with sp.Else():
                with sp.Fori(0, FULL // H) as n:
                    for s in range(H):
                        sp.wait_ge(slow_elu, n * H + s + 1)
                        sp.dma_start(e_buf[:, 0, :], z_dram[ds(n, 1), :, s * GE:(s + 1) * GE].rearrange("n p f -> (n p) f")).then_inc(slow_in, 16)
                sp.wait_ge(slow_elu, FULL + 1)
                sp.dma_start(e_buf[:, 0, 0:TAIL_E], z_dram[2 * TURNS, :, 0:TAIL_E]).then_inc(slow_in, 16)

            def store_res(it, s):
                wait(sp, res_ready, it * U3 + s + 1)
                sp.dma_start(out_full[:, ds(it * U3 + s, 1), :, :].rearrange("p n t c -> p (n t) c"),
                             z_buf[:, 2 + s, :].rearrange("p (t c) -> p t c", c=C)).then_inc(res_out[s], 16)

            with sp.Fori(0, TURNS3) as it:
                for s in range(U3):
                    store_res(it, s)
            sp.wait_ge(res_ready, CHF + 1)
            sp.dma_start(out[CHF * CH:N, :], z_buf[0:CH_TAIL, 2, 0:C]).then_inc(res_out[0], 16)
            sp.wait_ge(res_out[0], 16 * (TURNS3 + 1))
            sp.wait_ge(res_out[1], 16 * TURNS3)

        @block.gpsimd
        def _(pool):
            pool.memset(x_sb[:, NT - 1, :], 0.0).then_inc(x_cleared, 1)
            pool.memset(dst_raw[:, BLK - 1, :], 0).then_inc(idx_cleared, 1)
            pool.memset(src_raw[:, BLK - 1, :], 0).then_inc(idx_cleared, 1)
            pool.memset(ident[:, :], 0.0).then_inc(ident_zero, 1)
            pool.memset(ones_bf[:, :], 1.0).then_inc(consts_ready, 1)
            for const, value in ((minus_half, -0.5), (minus_one, -1.0), (ln_eps, LN_EPS)):
                pool.memset(const[:, :], value).then_inc(consts_ready, 1)
            pool.iota(iota[:, :], [[1, SWIN]], base=0, channel_multiplier=0,
                      allow_small_or_imprecise_dtypes=True).then_inc(consts_ready, 1)
            pool.wait_ge(ident_zero, 1)
            pool.affine_select(out=ident[:, :], in_=ident[:, :], compare_op=ALU.not_equal, fill=1.0,
                               base=0, pattern=[[-1, P]], channel_multiplier=1).then_inc(consts_ready, 1)
            pool.wait_ge(consts_ready, 6)
            pool.wait_ge(src_in, 64)
            pool.tensor_copy(src_f, src_raw).then_inc(idx_float, 1)
            def turn_a(it):
                pool.wait_ge(ln_step, (it + 1) * LT)
                wait(pool, h_ready, it)
                pool.tensor_tensor(rstd[:, :], ln_mv[:, :, 1], ln_eps[:, :], ALU.add).then_inc(ln_root, 1)
                pool.wait_ge(ln_root, 3 * it + 1)
                pool.tensor_tensor(rstd[:, :], rstd[:, :], minus_half[:, :], ALU.pow).then_inc(ln_root, 1)
                pool.wait_ge(ln_root, 3 * it + 2)
                pool.tensor_tensor(ln_bias[:, :], ln_mv[:, :, 0], rstd[:, :], ALU.mult).then_inc(ln_root, 1)
                pool.wait_ge(ln_root, 3 * it + 3)
                pool.tensor_tensor(ln_bias[:, :], ln_bias[:, :], minus_one[:, :], ALU.mult).then_inc(ln_ready, 1)
                pool.wait_ge(hT_copied, it + 1)
                pool.tensor_copy(hT[:, ds(it * LT * P, LT * P)], hT_st).then_inc(hT_saved, 1)
            node_turns(pool, turn_a)
            pool.wait_ge(idx_kept, 3 * BLK)
            pool.memset(agg_flat, 0.0).then_inc(table_cleared, 1)

            def take_indices(it, h, n):
                for s in range(h * H, h * H + H):
                    wait(pool, g_in[s], 16 * K * it)
                pool.tensor_copy(idx_now[:, h * H:h * H + n, :], src_idx[:, ds(count(it, h * H), n), :]).then_inc(idx_copied, 1)

            def gather(s, rows):
                for k in range(K):
                    pool.indirect_dma_start(
                        out=g_buf[0:rows, s, k * C:(k + 1) * C], out_offset=None,
                        in_=p_dram[:, :],
                        in_offset=bass.IndirectOffsetOnAxis(ap=idx_now[0:rows, s, k:k + 1].bitcast(U32), axis=0),
                    ).then_inc(g_in[s], 16)

            def turn_b(it):
                for h in range(2):
                    pool.wait_ge(idx_copied, 2 * it + h + 1)
                    wait(pool, z_ready, count(it - 1, h * H + H))
                    if isinstance(it, int) and it == TURNS - 1 and h == 1:
                        take_indices(TURNS, 0, 1)
                    else:
                        take_indices(*norm(it, h + 1, 2), H)
                    for s in range(h * H, h * H + H):
                        gather(s, P)

            pool.wait_ge(p_out, 16 * LTURNS)
            take_indices(0, 0, H)
            edge_turns(pool, turn_b)
            pool.wait_ge(idx_copied, 2 * TURNS + 1)
            pool.wait_ge(z_ready, count(TURNS - 1, 1))
            gather(0, TAIL_ROWS)

            pool.wait_ge(bn_step, 1)
            pool.tensor_scalar(bn_k[:, 0:1], bn_mv[:, 1:2], BN_EPS, None, ALU.add).then_inc(bn_root, 1)
            pool.wait_ge(bn_root, 1)
            pool.tensor_tensor(bn_k[:, 0:1], bn_k[:, 0:1], minus_half[:, 0:1], ALU.pow).then_inc(bn_root, 1)

            def add_window(it, s):
                n = count(it, s)
                base = pool.value_load(base_row[0:1, ds(n, 1)], min_val=0, max_val=N - 1)
                wait(pool, win_copied, n + 1)
                wait(pool, win_added, n)
                table = agg[:, :, ds(base, WIN)]
                pool.tensor_tensor(table, table, win_sum[:, s % 2, :, :], ALU.add).then_inc(win_added, 1)

            def turn_c(it):
                for s in range(U):
                    before, slot = norm(it, s - 2, U)
                    if exists(before):
                        add_window(before, slot)

            pool.wait_ge(flag_ready, 1)
            pool.wait_ge(base_in, 16)
            wide = pool.value_load(flag[0:1, 0:1], min_val=0, max_val=N)
            with pool.If(wide < WIN):
                edge_turns(pool, turn_c)
                for s in range(-2, 1):
                    add_window(*norm(TURNS, s, U))
                pool.wait_ge(win_added, GROUPS)
                pool.engine_nop().then_inc(agg_done, 1)
            with pool.Else():
                pool.wait_ge(slow_added, GROUPS * NWIN + 1)
                pool.engine_nop().then_inc(agg_done, 1)

            pool.wait_ge(bn_step, 6)
            pool.tensor_scalar(bn2_k[:, 0:1], bn2_mv[:, 1:2], BN_EPS, None, ALU.add).then_inc(bn_root, 1)
            pool.wait_ge(bn_root, 3)
            pool.tensor_tensor(bn2_k[:, 0:1], bn2_k[:, 0:1], minus_half[:, 0:1], ALU.pow).then_inc(bn_root, 1)

        @block.tensor
        def _(pe):
            pe.wait_ge(consts_ready, 6)
            pe.wait_ge(w_in, 32)
            for i, w in enumerate((w1_sb, w2_sb)):
                for j in range(2):
                    last = pe.transpose(ps[:, 6, (2 * i + j) * C:(2 * i + j + 1) * C], w[:, j * C:(j + 1) * C], ident[:, :])
            last.then_inc(w_turned, 1)

            n = 0
            for what, ready, value in ((rel_f, rel_ready, BLK), (dst_f, rel_ready, BLK), (src_f, idx_float, 2)):
                pe.wait_ge(ready, value)
                for j in range(BLK):
                    if n == 1:
                        pe.wait_ge(wT_ready, 1)
                    if n >= 2:
                        pe.wait_ge(idx_kept, n - 1)
                    for k in range(K):
                        last = pe.transpose(ps[:, 7 - n % 2, k * P:(k + 1) * P], what[:, j, k:GE:K], ident[:, :])
                    last.then_inc(idx_turned, 1)
                    n += 1
            pe.wait_ge(span_step, 2)
            pe.wait_ge(idx_kept, n)
            pe.transpose(ps[0:1, 6, 0:P], dspan1[:, 0:1], ident[:, :]).then_inc(span_turned, 1)

            tr_bank = ps[:, 0:2, :].rearrange("p a b -> p (a b)")
            p_bank = ps[:, 2:4, :].rearrange("p a b -> p (a b)")
            pe.wait_ge(wT_ready, 1)
            def turn_a(it):
                pe.wait_ge(h_ready, it + 1)
                wait(pe, hT_copied, it)
                for t in range(LT):
                    last = pe.transpose(tr_bank[:, t * P:(t + 1) * P], h_st[:, t * P:(t + 1) * P], ident[:, :])
                last.then_inc(h_turned, 1)
                pe.wait_ge(hT_copied, it + 1)
                wait(pe, p_added, it)
                for t in range(LT):
                    last = pe.matmul(p_bank[:, t * P:(t + 1) * P], hT_st[:, t * P:(t + 1) * P], wT[:, 0, :], start=True, stop=True)
                last.then_inc(p_product, 1)
            node_turns(pe, turn_a)
            pe.wait_ge(p_added, LTURNS)

            def turn_edges(it, s, rows):
                n = count(it, s)
                if s % H == 0:
                    pe.wait_ge(e_in[s // H], 16 * (it + 1))
                wait(pe, eT_ready, n - NPS + 1)
                for k in range(K):
                    last = pe.transpose(edge_bank[s % NPS][:, k * rows:(k + 1) * rows],
                                        e_buf[0:rows, s, k * C:(k + 1) * C], ident[0:rows, 0:rows])
                last.then_inc(e_turned, 1)

            def product(it, s, rows):
                n = count(it, s)
                bank = z_bank[s % NPS]
                pe.wait_ge(eT_ready, n + 1)
                wait(pe, z_saved, n - NPS + 1)
                pe.matmul(bank[:, 0:K * rows], wT[:, 1, :], t_buf[:, s % NPS, 0:K * rows], start=True, stop=False)
                pe.wait_ge(g_in[s], 16 * K * (it + 1))
                for k in range(K):
                    last = pe.matmul(bank[:, k * rows:(k + 1) * rows], g_buf[0:rows, s, k * C:(k + 1) * C],
                                     ident[0:rows, 0:rows], start=False, stop=(k == K - 1))
                last.then_inc(z_ready, 1)

            def turn_b(it):
                for s in range(U):
                    if s + 1 < U or not (isinstance(it, int) and it == TURNS - 1):
                        turn_edges(*norm(it, s + 1, U), P)
                    else:
                        turn_edges(TURNS, 0, TAIL_ROWS)
                    product(it, s, P)

            turn_edges(0, 0, P)
            edge_turns(pe, turn_b)
            product(TURNS, 0, TAIL_ROWS)
            pe.wait_ge(z_saved, GROUPS)

            def turn_elu(it, s, rows):
                n = count(it, s)
                pe.wait_ge(elu_ready, n + 1)
                wait(pe, elu_edges, n - NPS + 1)
                for k in range(K):
                    last = pe.transpose(edge_bank[s % NPS][0:rows, k * C:(k + 1) * C],
                                        z_buf[:, s % NPS, k * rows:(k + 1) * rows], ident[:, :])
                last.then_inc(elu_turned, 1)

            def windows(it, s, rows):
                n = count(it, s)
                bank = win_bank[s % 2]
                pe.wait_ge(elu_edges, n + 1)
                pe.wait_ge(hot_ready, n + 1)
                wait(pe, win_copied, n - 1)
                hot_bf = one_hot[0:rows, s % NPS, :, :].bitcast(BF16)
                for k in range(K):
                    pe.matmul(bank[:, 0:WIN], g_buf[0:rows, s % NPS, k * C:(k + 1) * C], one_hot[0:rows, s % NPS, k, :],
                              start=(k == 0), stop=(k == K - 1))
                for k in range(K):
                    last = pe.matmul(bank[:, WIN:2 * WIN], ones_bf[0:rows, :], hot_bf[:, k, 1:2 * WIN:2],
                                     start=(k == 0), stop=(k == K - 1))
                last.then_inc(win_ready, 1)

            def turn_c(it):
                for s in range(U):
                    turn_elu(it, s, P)
                    before, slot = norm(it, s - 1, U)
                    if exists(before):
                        windows(before, slot, P)

            pe.wait_ge(flag_ready, 1)
            wide = pe.value_load(flag[0:1, 0:1], min_val=0, max_val=N)
            with pe.If(wide < WIN):
                edge_turns(pe, turn_c)
                turn_elu(TURNS, 0, TAIL_ROWS)
                windows(TURNS - 1, U - 1, P)
                windows(TURNS, 0, TAIL_ROWS)
            with pe.Else():
                def slow_group(n, rows):
                    pe.wait_ge(slow_elu, n + 2)
                    for k in range(K):
                        last = pe.transpose(edge_bank[0][0:rows, k * C:(k + 1) * C],
                                            z_buf[:, 0, k * rows:(k + 1) * rows], ident[:, :])
                    last.then_inc(slow_turned, 1)
                    with pe.Fori(0, NWIN) as w:
                        pe.wait_ge(slow_edges, n + 1)
                        step = n * NWIN + w
                        pe.wait_ge(slow_hot, step + 1)
                        pe.wait_ge(slow_added, step + 1)
                        hot = z_buf[0:rows, 2:2 + K, :]
                        for k in range(K):
                            pe.matmul(win_bank[0][:, :], g_buf[0:rows, 0, k * C:(k + 1) * C], hot[:, k, :],
                                      start=(k == 0), stop=(k == K - 1))
                        for k in range(K):
                            last = pe.matmul(win_bank[1][:, :], ones_bf[0:rows, :], hot[:, k, :].bitcast(BF16)[:, 1:2 * SWIN:2],
                                             start=(k == 0), stop=(k == K - 1))
                        last.then_inc(slow_win, 1)
                with pe.Fori(0, FULL) as n:
                    slow_group(n, P)
                slow_group(FULL, TAIL_ROWS)

            def node_product(it, s, cols):
                n = it * U3 + s
                pe.wait_ge(mean_ready, n + 1)
                wait(pe, y_kept, n - 1)
                cs = ds(n * CH, cols)
                pe.matmul(edge_bank[s][:, 0:cols], wT[:, 2, :], hT[:, cs], start=True, stop=False)
                pe.matmul(edge_bank[s][:, 0:cols], wT[:, 3, :], t_buf[:, s, 0:cols], start=False, stop=True).then_inc(y_ready, 1)

            def turn_nodes(it, s, cols):
                n = it * U3 + s
                pe.wait_ge(yelu_ready, n + 1)
                wait(pe, res_ready, n - 1)
                for t in range(-(-cols // P)):
                    rows = min(P, cols - t * P)
                    last = pe.transpose(z_bank[s][0:rows, t * C:(t + 1) * C], g_buf[:, 2 + s, t * P:t * P + rows], ident[:, :])
                last.then_inc(yelu_turned, 1)

            for step in (node_product, turn_nodes):
                for s in range(U3):
                    step(0, s, CH)
                with pe.Fori(1, TURNS3) as it:
                    for s in range(U3):
                        step(it, s, CH)
                step(TURNS3, 0, CH_TAIL)

        @block.scalar
        def _(act):
            for n in range(3 * BLK):
                what, j = n // BLK, n % BLK
                kept = (rel_dst, abs_dst, src_idx)[what]
                act.wait_ge(idx_turned, n + 1)
                act.activation(kept[:, j * P:(j + 1) * P, :].rearrange("p g k -> p k g"),
                               ps[:, 7 - n % 2, :].rearrange("p (k g) -> p k g", k=K), ACT.Copy).then_inc(idx_kept, 1)
            def turn_a(it):
                act.wait_ge(ln_ready, it + 1)
                wait(act, h_turned, it)
                for t in range(LT):
                    last = act.activation(h_st[:, t * P:(t + 1) * P], x_sb[:, ds(it * LT + t, 1), :].rearrange("p n c -> p (n c)"),
                                          ACT.Relu, bias=ln_bias[:, t:t + 1], scale=rstd[:, t:t + 1])
                last.then_inc(h_ready, 1)

            node_turns(act, turn_a)

            def keep_eT(it, s, rows):
                n = count(it, s)
                act.wait_ge(e_turned, n + 1)
                wait(act, z_ready, n - NPS + 1)
                act.activation(t_buf[:, s % NPS, 0:K * rows], edge_bank[s % NPS][:, 0:K * rows], ACT.Copy).then_inc(eT_ready, 1)

            def keep_z(it, s, rows):
                n = count(it, s)
                act.wait_ge(z_ready, n + 1)
                if s % H == 0:
                    wait(act, z_out[s // H], 16 * it)
                wait(act, z_counted, n - U + 1)
                act.activation(z_buf[:, s, 0:K * rows], z_bank[s % NPS][:, 0:K * rows], ACT.Copy).then_inc(z_saved, 1)

            def turn_b(it):
                for s in range(U):
                    keep_eT(it, s, P)
                    before, slot = norm(it, s - 1, U)
                    if exists(before):
                        keep_z(before, slot, P)

            edge_turns(act, turn_b)
            keep_eT(TURNS, 0, TAIL_ROWS)
            keep_z(TURNS - 1, U - 1, P)
            keep_z(TURNS, 0, TAIL_ROWS)

            def exponent(it, s, rows):
                n = count(it, s)
                if s % H == 0:
                    act.wait_ge(z_in[s // H], 16 * (it + 1))
                wait(act, elu_ready, n - NPS + 1)
                act.activation(t_buf[:, s % NPS, 0:K * rows], e_buf[:, s, 0:K * rows], ACT.Exp,
                               bias=bn_k[:, 3:4], scale=bn_k[:, 1:2]).then_inc(exp_ready, 1)

            def keep_elu(it, s, rows):
                n = count(it, s)
                act.wait_ge(elu_turned, n + 1)
                wait(act, win_ready, n - NPS + 1)
                act.activation(g_buf[0:rows, s % NPS, :], edge_bank[s % NPS][0:rows, :], ACT.Copy).then_inc(elu_edges, 1)

            def turn_c(it):
                for s in range(U):
                    exponent(it, s, P)
                    before, slot = norm(it, s - 1, U)
                    if exists(before):
                        keep_elu(before, slot, P)

            act.wait_ge(flag_ready, 1)
            wide = act.value_load(flag[0:1, 0:1], min_val=0, max_val=N)
            act.wait_ge(bn1_ready, 1)
            with act.If(wide < WIN):
                edge_turns(act, turn_c)
                exponent(TURNS, 0, TAIL_ROWS)
                keep_elu(TURNS - 1, U - 1, P)
                keep_elu(TURNS, 0, TAIL_ROWS)
            with act.Else():
                def slow_group(n, rows):
                    act.wait_ge(slow_in, 16 * (n + 1))
                    act.activation(t_buf[:, 0, 0:K * rows], e_buf[:, 0, 0:K * rows], ACT.Exp,
                                   bias=bn_k[:, 3:4], scale=bn_k[:, 1:2]).then_inc(slow_exp, 1)
                    act.wait_ge(slow_turned, n + 2)
                    act.wait_ge(slow_win, n * NWIN + 1)
                    act.activation(g_buf[0:rows, 0, :], edge_bank[0][0:rows, :], ACT.Copy).then_inc(slow_edges, 1)
                with act.Fori(0, FULL) as n:
                    slow_group(n, P)
                slow_group(FULL, TAIL_ROWS)

            def keep_y(it, s, cols):
                n = it * U3 + s
                act.wait_ge(y_ready, n + 1)
                act.activation(hT[:, ds(n * CH, cols)], edge_bank[s][:, 0:cols], ACT.Identity, bias=vecs[:, 2:3]).then_inc(y_kept, 1)

            def node_exponent(it, s, cols):
                n = it * U3 + s
                wait(act, yelu_ready, n - 1)
                act.activation(t_buf[:, s, 0:cols], hT[:, ds(n * CH, cols)], ACT.Exp,
                               bias=bn2_k[:, 3:4], scale=bn2_k[:, 1:2]).then_inc(yexp_ready, 1)

            for step in (keep_y, node_exponent):
                if step is node_exponent:
                    act.wait_ge(bn2_ready, 1)
                for s in range(U3):
                    step(0, s, CH)
                with act.Fori(1, TURNS3) as it:
                    for s in range(U3):
                        step(it, s, CH)
                step(TURNS3, 0, CH_TAIL)

        @block.vector
        def _(dve):
            dve.wait_ge(dst_in, 64)
            dve.tensor_copy(dst_f, dst_raw).then_inc(idx_float, 1)
            dve.wait_ge(idx_float, 1)
            dve.wait_ge(idx_float, 2)
            dve.tensor_reduce(dmin[:, :], dst_f, AX_X, ALU.min).then_inc(dminmax, 1)
            dve.tensor_reduce(dmax[:, :], dst_f, AX_X, ALU.max).then_inc(dminmax, 1)
            dve.wait_ge(dminmax, 2)
            for j in range(BLK):
                dve.tensor_scalar(rel_f[:, j, :], dst_f[:, j, :], dmin[:, j:j + 1], None, ALU.subtract).then_inc(rel_ready, 1)
            dve.tensor_copy(base_i[:, :], dmin[:, :]).then_inc(base_ready, 1)
            dve.tensor_tensor(dspan[:, :], dmax[:, :], dmin[:, :], ALU.subtract).then_inc(span_step, 1)
            dve.wait_ge(span_step, 1)
            dve.tensor_reduce(dspan1[:, :], dspan[:, :], AX_X, ALU.max).then_inc(span_step, 1)
            dve.wait_ge(w_turned, 1)
            dve.tensor_copy(wT[:, :, :].rearrange("p a b -> p (a b)"), ps[:, 6, :]).then_inc(wT_ready, 1)
            dve.wait_ge(x_in, 32)
            tr_bank = ps[:, 0:2, :].rearrange("p a b -> p (a b)")
            p_bank = ps[:, 2:4, :].rearrange("p a b -> p (a b)")
            def layer_statistics(it):
                wait(dve, ln_ready, it)
                for t in range(LT):
                    dve.bn_stats(ln_st[:, t, :], x_sb[:, ds(it * LT + t, 1), :].rearrange("p n c -> p (n c)"))
                dve.drain()
                for t in range(LT):
                    dve.bn_aggr(ln_mv[:, t, :], ln_st[:, t, :]).then_inc(ln_step, 1)

            def node_table(it):
                dve.wait_ge(h_turned, it + 1)
                wait(dve, hT_saved, it)
                wait(dve, p_product, it)
                dve.tensor_copy(hT_st, tr_bank[:, 0:LT * P]).then_inc(hT_copied, 1)
                dve.wait_ge(p_product, it + 1)
                wait(dve, p_out, 16 * it)
                dve.tensor_tensor(p_st.rearrange("p (t c) -> p t c", c=C), p_bank[:, 0:LT * P].rearrange("p (t c) -> p t c", c=C),
                                  b1_rows[:, :].unsqueeze(1).to_broadcast([P, LT, C]), ALU.add).then_inc(p_added, 1)

            def turn_a(it):
                layer_statistics(it + 1)
                node_table(it)

            layer_statistics(0)
            dve.wait_ge(vec_in, 16 * 6)
            node_turns(dve, turn_a, last=LTURNS - 1)
            node_table(LTURNS - 1)
            dve.wait_ge(span_turned, 1)
            dve.tensor_reduce(span_all[:, :], ps[0:1, 6, 0:P], AX_X, ALU.max).then_inc(span_step, 1)
            dve.wait_ge(span_step, 3)
            dve.tensor_copy(flag[:, :], span_all[:, :]).then_inc(flag_ready, 1)

            def statistics(it, s, rows):
                n = count(it, s)
                dve.wait_ge(z_saved, n + 1)
                dve.bn_stats(stats[:, ds(n, 1), :].rearrange("p n f -> p (n f)"), z_buf[:, s, 0:K * rows]).then_inc(z_counted, 1)

            def turn_b(it):
                for s in range(U):
                    statistics(it, s, P)

            edge_turns(dve, turn_b)
            statistics(TURNS, 0, TAIL_ROWS)

            def bn_constants(mv, k, weight, bias, first, root):
                dve.wait_ge(bn_root, root)
                dve.tensor_tensor(k[:, 1:2], k[:, 0:1], weight, ALU.mult).then_inc(bn_step, 1)
                dve.wait_ge(bn_step, first + 1)
                dve.tensor_tensor(k[:, 2:3], mv[:, 0:1], k[:, 1:2], ALU.mult).then_inc(bn_step, 1)
                dve.wait_ge(bn_step, first + 2)
                dve.tensor_tensor(k[:, 3:4], bias, k[:, 2:3], ALU.subtract).then_inc(bn_step, 1)
                dve.wait_ge(bn_step, first + 3)
                dve.tensor_scalar(k[:, 4:5], k[:, 3:4], 1.0, None, ALU.add).then_inc(bn_step, 1)
                dve.wait_ge(bn_step, first + 4)

            dve.wait_ge(z_counted, GROUPS)
            dve.bn_aggr(bn_mv[:, :], stats[:, :, :].rearrange("p n f -> p (n f)")).then_inc(bn_step, 1)
            bn_constants(bn_mv, bn_k, vecs[:, 0:1], vecs[:, 1:2], 1, 2)
            dve.engine_nop().then_inc(bn1_ready, 1)
            dve.wait_ge(z_out[0], 16 * (TURNS + 1))
            dve.wait_ge(z_out[1], 16 * TURNS)

            def elu(it, s, rows):
                n = count(it, s)
                line = z_buf[:, s % NPS, 0:K * rows]
                if s % H == 0:
                    dve.wait_ge(z_in[s // H], 16 * (it + 1))
                wait(dve, elu_turned, n - NPS + 1)
                dve.tensor_scalar(line, e_buf[:, s, 0:K * rows], bn_k[:, 1:2], bn_k[:, 4:5], ALU.mult, ALU.add).then_inc(lin_ready, 1)
                dve.wait_ge(lin_ready, n + 1)
                dve.wait_ge(exp_ready, n + 1)
                dve.scalar_tensor_tensor(out=line, in0=t_buf[:, s % NPS, 0:K * rows], scalar=1.0, in1=line,
                                         op0=ALU.min, op1=ALU.max).then_inc(elu_ready, 1)

            def hot(it, s, rows):
                n = count(it, s)
                wait(dve, win_ready, n - NPS + 1)
                dve.tensor_tensor(
                    one_hot[0:rows, s % NPS, :, :],
                    rel_dst[0:rows, ds(n, 1), :].rearrange("p n k -> p (n k)").unsqueeze(2).to_broadcast([rows, K, WIN]),
                    iota[0:rows, 0:WIN].unsqueeze(1).to_broadcast([rows, K, WIN]),
                    ALU.is_equal).then_inc(hot_ready, 1)

            def copy_window(it, s):
                n = count(it, s)
                dve.wait_ge(win_ready, n + 1)
                wait(dve, win_added, n - 1)
                dve.tensor_copy(win_sum[:, s % 2, :, :].rearrange("p a w -> p (a w)"), win_bank[s % 2][:, 0:2 * WIN]).then_inc(win_copied, 1)

            def turn_c(it):
                for s in range(U):
                    hot(it, s, P)
                    elu(it, s, P)
                    before, slot = norm(it, s - 2, U)
                    if exists(before):
                        copy_window(before, slot)

            dve.wait_ge(table_cleared, 1)
            wide = dve.value_load(flag[0:1, 0:1], min_val=0, max_val=N)
            with dve.If(wide < WIN):
                edge_turns(dve, turn_c)
                hot(TURNS, 0, TAIL_ROWS)
                elu(TURNS, 0, TAIL_ROWS)
                for s in range(-2, 1):
                    copy_window(*norm(TURNS, s, U))
            with dve.Else():
                for ahead in (slow_elu, slow_turned, slow_win, slow_added):
                    dve.engine_nop().then_inc(ahead, 1)

                def slow_group(n, rows):
                    line = z_buf[:, 0, 0:K * rows]
                    now = one_hot[:, 0, 0, 0:K]
                    dve.wait_ge(slow_in, 16 * (n + 1))
                    dve.wait_ge(slow_turned, n + 1)
                    dve.tensor_scalar(line, e_buf[:, 0, 0:K * rows], bn_k[:, 1:2], bn_k[:, 4:5], ALU.mult, ALU.add).then_inc(slow_lin, 1)
                    dve.wait_ge(slow_lin, n + 1)
                    dve.wait_ge(slow_exp, n + 1)
                    dve.scalar_tensor_tensor(out=line, in0=t_buf[:, 0, 0:K * rows], scalar=1.0, in1=line,
                                             op0=ALU.min, op1=ALU.max).then_inc(slow_elu, 1)
                    dve.tensor_copy(now, abs_dst[:, ds(n, 1), :].rearrange("p n k -> p (n k)")).then_inc(slow_dst, 1)
                    with dve.Fori(0, NWIN) as w:
                        step = n * NWIN + w
                        dve.wait_ge(slow_dst, n * (NWIN + 1) + w + 1)
                        dve.wait_ge(slow_win, step + 1)
                        for k in range(K):
                            last = dve.tensor_scalar(z_buf[:, 2 + k, :], iota[:, :], now[:, k:k + 1], None, ALU.is_equal)
                        last.then_inc(slow_hot, 1)
                        dve.wait_ge(slow_hot, step + 1)
                        dve.tensor_scalar(now, now, float(SWIN), None, ALU.subtract).then_inc(slow_dst, 1)
                        dve.wait_ge(slow_win, step + 2)
                        table = agg[:, :, ds(w * SWIN, SWIN)]
                        dve.tensor_tensor(table, table, ps[:, 6:8, :], ALU.add).then_inc(slow_added, 1)
                        dve.wait_ge(slow_added, step + 2)
                with dve.Fori(0, FULL) as n:
                    slow_group(n, P)
                slow_group(FULL, TAIL_ROWS)

            def mean(it, s, cols):
                n = it * U3 + s
                cs = ds(n * CH, cols)
                cnt = z_buf[:, s, 0:cols]
                dif = z_buf[:, 4 + s, 0:cols]
                wait(dve, y_ready, n - 1)
                dve.tensor_scalar(cnt, agg[:, 1, cs], 1.0, None, ALU.max).then_inc(mean_step, 1)
                dve.tensor_tensor(dif, agg[:, 0, cs], agg[:, 1, cs], ALU.subtract).then_inc(mean_step, 1)
                dve.wait_ge(mean_step, 3 * n + 2)
                dve.reciprocal(cnt, cnt).then_inc(mean_step, 1)
                dve.wait_ge(mean_step, 3 * n + 3)
                dve.tensor_tensor(t_buf[:, s, 0:cols], dif, cnt, ALU.mult).then_inc(mean_ready, 1)

            def node_statistics(it, s, cols):
                n = it * U3 + s
                dve.wait_ge(y_kept, n + 1)
                dve.bn_stats(stats2[:, ds(n, 1), :].rearrange("p n f -> p (n f)"), hT[:, ds(n * CH, cols)]).then_inc(y_counted, 1)

            def node_elu(it, s, cols):
                n = it * U3 + s
                line = g_buf[:, 2 + s, 0:cols]
                wait(dve, yelu_turned, n - 1)
                dve.tensor_scalar(line, hT[:, ds(n * CH, cols)], bn2_k[:, 1:2], bn2_k[:, 4:5], ALU.mult, ALU.add).then_inc(ylin_ready, 1)
                dve.wait_ge(ylin_ready, n + 1)
                dve.wait_ge(yexp_ready, n + 1)
                dve.scalar_tensor_tensor(out=line, in0=t_buf[:, s, 0:cols], scalar=1.0, in1=line,
                                         op0=ALU.min, op1=ALU.max).then_inc(yelu_ready, 1)

            def residual(it, s, cols):
                n = it * U3 + s
                tiles = -(-cols // P)
                rows = min(P, cols)
                dve.wait_ge(yelu_turned, n + 1)
                wait(dve, res_out[s], 16 * it)
                dve.scalar_tensor_tensor(out=z_buf[0:rows, 2 + s, 0:tiles * C], in0=z_bank[s][0:rows, 0:tiles * C], scalar=-1.0,
                                         in1=x_sb[0:rows, ds(n * (CH // P), tiles), :].rearrange("p t c -> p (t c)"),
                                         op0=ALU.add, op1=ALU.add).then_inc(res_ready, 1)

            dve.wait_ge(agg_done, 1)
            for first, second in ((mean, node_statistics), (node_elu, residual)):
                first(0, 0, CH)
                first(0, 1, CH)
                second(0, 0, CH)
                with dve.Fori(1, TURNS3) as it:
                    first(it, 0, CH)
                    second(it - 1, 1, CH)
                    first(it, 1, CH)
                    second(it, 0, CH)
                first(TURNS3, 0, CH_TAIL)
                second(TURNS3 - 1, 1, CH)
                second(TURNS3, 0, CH_TAIL)
                if first is mean:
                    dve.wait_ge(y_counted, CHF + 1)
                    dve.bn_aggr(bn2_mv[:, :], stats2[:, :, :].rearrange("p n f -> p (n f)")).then_inc(bn_step, 1)
                    bn_constants(bn2_mv, bn2_k, vecs[:, 3:4], vecs[:, 4:5], 6, 4)
                    dve.engine_nop().then_inc(bn2_ready, 1)


_INS = ["x", "src", "dst", "edge_attr_128", "L0_gnn_w1", "L0_gnn_b1", "L0_gnn_bn1_w", "L0_gnn_bn1_b",
        "L0_gnn_w2", "L0_gnn_b2", "L0_gnn_bn2_w", "L0_gnn_bn2_b"]


def kernel(**inputs):
    import numpy as _np
    import concourse.bacc as _bacc
    from concourse import mybir as _mybir
    from concourse.bass_utils import run_bass_kernel_spmd as _run

    nc = _bacc.Bacc("TRN2", target_bir_lowering=False, num_devices=1)
    arrays, args = {}, []
    for name in _INS:
        a = _np.ascontiguousarray(inputs[name])
        arrays[f"in_{name}"] = a
        args.append(nc.dram_tensor(f"in_{name}", a.shape, _mybir.dt.from_np(a.dtype), kind="ExternalInput").ap())
    shape = inputs["x"].shape
    args.append(nc.dram_tensor("out_0", shape, _mybir.dt.float32, kind="ExternalOutput").ap())
    gnn_kernel(nc, *args)
    r = _run(nc, [arrays], core_ids=[0])
    return r.results[0]["out_0"]
```

```python
from contextlib import ExitStack

import concourse.bass as bass
from concourse import mybir

F32 = mybir.dt.float32
BF16 = mybir.dt.bfloat16
I32 = mybir.dt.int32
U32 = mybir.dt.uint32
ALU = mybir.AluOpType
ACT = mybir.ActivationFunctionType
AX_X = mybir.AxisListType.X
ds = bass.ds

P = 128
K = 4
GE = P * K
U = 12
H = 3
CU = U // H
EB = 6
NPS = 3
PU = U // 2
WIN = 48
WARM = 96
BANK = 512
LN_EPS = 1e-5
BN_EPS = 1e-5
LT = 7


def wait(eng, sem, value):
    if isinstance(value, int) and value <= 0:
        return
    eng.wait_ge(sem, value)


def norm(it, s, unroll):
    return it + s // unroll, s % unroll


def exists(it):
    return not (isinstance(it, int) and it < 0)


def gnn_kernel(nc, x, src, dst, edge_attr, w1, b1, bn1_w, bn1_b, w2, b2, bn2_w, bn2_b, out):
    N, C = x.shape
    E = edge_attr.shape[0]
    assert C == P
    NT = -(-N // P)
    NP = NT * P
    N_LAST = N - (NT - 1) * P
    LTURNS = NT // LT
    assert LTURNS * LT == NT
    FULL = E // GE
    TURNS = FULL // U
    SHORT = FULL - TURNS * U
    assert TURNS >= 3 and SHORT == EB and FULL % H == 0
    TAIL_ROWS = (E - FULL * GE) // K
    assert 0 < TAIL_ROWS < P and FULL * GE + TAIL_ROWS * K == E
    GROUPS = FULL + 1
    BLK = -(-GROUPS // P)
    B_ROWS = FULL - (BLK - 1) * P
    TAIL_E = TAIL_ROWS * K
    TAIL = (TURNS, SHORT)
    CHUNKS = FULL // H
    SWIN = BANK
    NWIN = -(-N // SWIN)
    TABLE = max(NWIN * SWIN, N + WIN)
    CH = BANK
    CHF = N // CH
    U3 = 2
    TURNS3 = CHF // U3
    assert TURNS3 * U3 == CHF and TURNS3 >= 3
    CH_TAIL = N - CHF * CH
    assert CH_TAIL <= P

    p_dram = nc.dram_tensor("p_table", [NP, C], F32, kind="Internal").ap()
    z_dram = nc.dram_tensor("z_edges", [CHUNKS + 1, P, H * GE], F32, kind="Internal").ap()
    base_dram = nc.dram_tensor("base_row_dram", [BLK * P], I32, kind="Internal").ap()

    with ExitStack() as ctx:
        def sb(name, shape, dt=F32):
            return ctx.enter_context(nc.sbuf_tensor(name, shape, dt))

        def sem(name):
            return ctx.enter_context(nc.semaphore(name))

        ps = ctx.enter_context(nc.psum_tensor("ps", [P, 8, BANK], F32))

        ident = sb("ident", [P, P])
        ones_bf = sb("ones_bf", [P, P], BF16)
        minus_half = sb("minus_half", [P, LT])
        minus_one = sb("minus_one", [P, LT])
        ln_eps = sb("ln_eps", [P, LT])
        iota = sb("iota", [P, SWIN])
        w1_sb = sb("w1_sb", [P, 2 * C])
        w2_sb = sb("w2_sb", [P, 2 * C])
        wT = sb("wT", [P, 4, C])
        b1_rows = sb("b1_rows", [P, C])
        vecs = sb("vecs", [P, 5])
        x_sb = sb("x_sb", [P, NT, C])
        hT = sb("hT", [P, NP])
        agg = sb("agg", [P, 2, TABLE])
        agg_flat = agg[:, :, :].rearrange("p a n -> p (a n)")
        src_idx = sb("src_idx", [P, GROUPS, K], I32)
        rel_dst = sb("rel_dst", [P, GROUPS, K])
        abs_dst = sb("abs_dst", [P, GROUPS, K])
        base_row = sb("base_row", [1, BLK * P], I32)
        flag = sb("flag", [1, 1], I32)
        IB = BLK * GE
        assert 5 * IB <= 2 * TABLE
        raw = [agg_flat[:, i * IB:(i + 1) * IB] for i in range(5)]
        src_raw = raw[0].bitcast(I32).rearrange("p (j e) -> p j e", j=BLK)
        dst_raw = raw[1].bitcast(I32).rearrange("p (j e) -> p j e", j=BLK)
        src_f, dst_f, rel_f = [r.rearrange("p (j e) -> p j e", j=BLK) for r in raw[2:5]]
        dmin = sb("dmin", [P, BLK])
        dmax = sb("dmax", [P, BLK])
        dspan = sb("dspan", [P, BLK])
        dspan1 = sb("dspan1", [P, 1])
        span_all = sb("span_all", [1, 1])
        base_i = sb("base_i", [P, BLK], I32)
        ln_st = sb("ln_st", [P, LT, 6])
        ln_mv = sb("ln_mv", [P, LT, 2])
        rstd = sb("rstd", [P, LT])
        ln_bias = sb("ln_bias", [P, LT])
        edge_buf = sb("edge_buf", [P, 2 * EB + U + 4, GE])
        e_buf = edge_buf[:, 0:EB, :]
        z_buf = edge_buf[:, EB:2 * EB, :]
        g_buf = edge_buf[:, 2 * EB:2 * EB + U, :]
        t_buf = edge_buf[:, 2 * EB + U:, :]
        zi_buf = edge_buf[:, 0:U, :]
        f_buf = g_buf[:, 0:6, :]
        m_buf = g_buf[:, 6:12, :]
        x_buf = t_buf
        idx_now = sb("idx_now", [P, U, K], I32)
        hot_bf = sb("hot_bf", [P, NPS, K, WIN], BF16)
        one_hot = sb("one_hot", [P, NPS, 2, K, WARM])
        win_sum = sb("win_sum", [P, 2, 2, WIN])
        stats = sb("stats", [P, GROUPS, 6])
        bn_mv = sb("bn_mv", [P, 2])
        bn_k = sb("bn_k", [P, 5])
        stats2 = sb("stats2", [P, CHF + 1, 6])
        bn2_mv = sb("bn2_mv", [P, 2])
        bn2_k = sb("bn2_k", [P, 5])
        h_st = e_buf[:, 0:2, :].rearrange("p a b -> p (a b)")[:, 0:LT * P]
        hT_st = e_buf[:, 2:4, :].rearrange("p a b -> p (a b)")[:, 0:LT * P]
        p_st = e_buf[:, 4:6, :].rearrange("p a b -> p (a b)")[:, 0:LT * P]

        x_cleared = sem("x_cleared")
        x_first = sem("x_first")
        x_in = sem("x_in")
        w_in = sem("w_in")
        vec_in = sem("vec_in")
        idx_cleared = sem("idx_cleared")
        src_in = sem("src_in")
        dst_in = sem("dst_in")
        ident_zero = sem("ident_zero")
        consts_ready = sem("consts_ready")
        w_turned = sem("w_turned")
        wT_ready = sem("wT_ready")
        idx_float = sem("idx_float")
        dminmax = sem("dminmax")
        rel_ready = sem("rel_ready")
        base_ready = sem("base_ready")
        base_out = sem("base_out")
        base_in = sem("base_in")
        span_step = sem("span_step")
        span_turned = sem("span_turned")
        flag_ready = sem("flag_ready")
        idx_turned = sem("idx_turned")
        idx_kept = sem("idx_kept")
        table_cleared = sem("table_cleared")
        ln_step = sem("ln_step")
        ln_root = sem("ln_root")
        ln_ready = sem("ln_ready")
        h_ready = sem("h_ready")
        h_turned = sem("h_turned")
        hT_copied = sem("hT_copied")
        hT_saved = sem("hT_saved")
        p_product = sem("p_product")
        p_added = sem("p_added")
        p_out = sem("p_out")
        e_in = [sem(f"e_in{h}") for h in range(2)]
        z_out = [sem(f"z_out{h}") for h in range(2)]
        g_in = [sem(f"g_in{s}") for s in range(U)]
        idx_copied = sem("idx_copied")
        e_turned = sem("e_turned")
        eT_ready = sem("eT_ready")
        z_ready = sem("z_ready")
        z_counted = sem("z_counted")
        z_saved = sem("z_saved")
        bn_step = sem("bn_step")
        bn_root = sem("bn_root")
        bn1_ready = sem("bn1_ready")
        cnt_hot = sem("cnt_hot")
        cnt_ready = sem("cnt_ready")
        cnt_added = sem("cnt_added")
        counts_cleared = sem("counts_cleared")
        z_in = [sem(f"z_in{c}") for c in range(CU)]
        exp_ready = sem("exp_ready")
        lin_ready = sem("lin_ready")
        elu_ready = sem("elu_ready")
        elu_turned = sem("elu_turned")
        elu_edges = sem("elu_edges")
        hot_cleared = sem("hot_cleared")
        hot_ready = sem("hot_ready")
        win_ready = sem("win_ready")
        win_copied = sem("win_copied")
        win_added = sem("win_added")
        slow_in = sem("slow_in")
        slow_exp = sem("slow_exp")
        slow_lin = sem("slow_lin")
        slow_elu = sem("slow_elu")
        slow_turned = sem("slow_turned")
        slow_edges = sem("slow_edges")
        slow_dst = sem("slow_dst")
        slow_hot = sem("slow_hot")
        slow_win = sem("slow_win")
        slow_added = sem("slow_added")
        agg_done = sem("agg_done")
        mean_step = sem("mean_step")
        mean_ready = sem("mean_ready")
        y_ready = sem("y_ready")
        y_kept = sem("y_kept")
        y_counted = sem("y_counted")
        bn2_ready = sem("bn2_ready")
        yexp_ready = sem("yexp_ready")
        ylin_ready = sem("ylin_ready")
        yelu_ready = sem("yelu_ready")
        yelu_turned = sem("yelu_turned")
        res_ready = sem("res_ready")
        res_out = [sem(f"res_out{s}") for s in range(U3)]

        e_full = edge_attr[0:FULL * GE, :].rearrange("(g p k) c -> p g (k c)", p=P, k=K)
        e_tail = edge_attr[FULL * GE:E, :].rearrange("(p k) c -> p (k c)", k=K)
        out_full = out[0:CHF * CH, :].rearrange("(n t p) c -> p n t c", p=P, t=CH // P)

        def count(it, s):
            return it * U + s

        edge_bank = [ps[:, b, :] for b in range(NPS)]
        z_bank = [ps[:, NPS + b, :] for b in range(NPS)]
        win_bank = [ps[:, 6 + b, :] for b in range(2)]

        def uses(it, s, depth):
            return it * (U // depth) + s // depth

        def edge_turns(eng, turn):
            turn(0, U)
            with eng.Fori(1, TURNS) as it:
                turn(it, U)
            turn(TURNS, SHORT)

        def node_turns(eng, turn, first=0, last=LTURNS):
            turn(first)
            with eng.Fori(first + 1, last) as it:
                turn(it)

        block = ctx.enter_context(nc.Block())

        @block.sync
        def _(sp):
            sp.dma_start(w1_sb[:, :], w1).then_inc(w_in, 16)
            sp.dma_start(w2_sb[:, :], w2).then_inc(w_in, 16)
            last_x = NT - 1
            sp.dma_start(x_sb[:, 0:LT, :], x[0:LT * P, :].rearrange("(t p) c -> p t c", p=P)).then_inc(x_first, 16)
            sp.dma_start(x_sb[:, LT:last_x, :], x[LT * P:last_x * P, :].rearrange("(t p) c -> p t c", p=P)).then_inc(x_in, 16)
            sp.wait_ge(x_cleared, 1)
            sp.dma_start(x_sb[0:N_LAST, last_x, :], x[last_x * P:N, :]).then_inc(x_in, 16)
            sp.wait_ge(idx_cleared, 2)
            b0 = (BLK - 1) * P * GE
            for raw_idx, ids, landed in ((dst_raw, dst, dst_in), (src_raw, src, src_in)):
                sp.dma_start(raw_idx[:, 0:BLK - 1, :], ids[0:b0].rearrange("(j g e) -> g j e", g=P, e=GE)).then_inc(landed, 16)
                sp.dma_start(raw_idx[0:B_ROWS, BLK - 1, :], ids[b0:FULL * GE].rearrange("(g e) -> g e", e=GE)).then_inc(landed, 16)
                sp.dma_start(raw_idx[B_ROWS:B_ROWS + 1, BLK - 1, 0:TAIL_E],
                             ids[FULL * GE:E].rearrange("(g e) -> g e", g=1)).then_inc(landed, 16)
                sp.dma_start(raw_idx[B_ROWS:B_ROWS + 1, BLK - 1, TAIL_E:GE],
                             ids[FULL * GE:FULL * GE + GE - TAIL_E].rearrange("(g e) -> g e", g=1)).then_inc(landed, 16)
            sp.dma_start(b1_rows[:, :], b1.partition_broadcast(P)).then_inc(vec_in, 16)
            for i, v in enumerate((bn1_w, bn1_b, b2, bn2_w, bn2_b)):
                sp.dma_start(vecs[:, i:i + 1], v.rearrange("(c o) -> c o", o=1)).then_inc(vec_in, 16)
            sp.wait_ge(base_ready, 1)
            sp.dma_start(base_dram.rearrange("(j g) -> g j", g=P), base_i[:, :], allow_slow_non_contiguous=True).then_inc(base_out, 16)
            sp.wait_ge(base_out, 16)
            sp.dma_start(base_row[:, :], base_dram.rearrange("(o g) -> o g", o=1)).then_inc(base_in, 16)
            p_view = p_dram.rearrange("(n t p) c -> p n t c", p=P, t=LT)
            def turn_a(it):
                sp.wait_ge(p_added, it + 1)
                sp.dma_start(p_view[:, ds(it, 1), :, :].rearrange("p n t c -> p (n t) c"),
                             p_st.rearrange("p (t c) -> p t c", c=C)).then_inc(p_out, 16)
            node_turns(sp, turn_a)
            sp.wait_ge(p_out, 16 * LTURNS)
            sp.wait_ge(hT_saved, LTURNS)

            def load_edges(it, c):
                n = count(it, c * H)
                half = c % 2
                wait(sp, e_turned, n - EB + H)
                sp.dma_start(e_buf[:, half * H:(half + 1) * H, :], e_full[:, ds(n, H), :]).then_inc(e_in[half], 16)

            def store_z(it, c):
                half = c % 2
                wait(sp, z_saved, count(it, c * H + H))
                sp.dma_start(z_dram[ds(it * CU + c, 1), :, :].rearrange("n p f -> (n p) f"),
                             z_buf[:, half * H:(half + 1) * H, :].rearrange("p a b -> p (a b)")).then_inc(z_out[half], 16)

            def turn_b(it, groups):
                for c in range(groups // H):
                    load_edges(it, c)
                    before, slot = norm(it, c - 2, CU)
                    if exists(before):
                        store_z(before, slot)

            edge_turns(sp, turn_b)
            n_tail = FULL // H % CU
            sp.wait_ge(e_turned, FULL - H)
            sp.dma_start(e_buf[0:TAIL_ROWS, 0, :], e_tail).then_inc(e_in[0], 16)
            for c in range(n_tail - 2, n_tail):
                store_z(TURNS, c)
            sp.wait_ge(z_saved, GROUPS)
            sp.dma_start(z_dram[CHUNKS, :, 0:TAIL_E], z_buf[:, 0, 0:TAIL_E]).then_inc(z_out[0], 16)
            sp.wait_ge(e_turned, GROUPS)
            sp.wait_ge(z_out[0], 16 * (CHUNKS // 2 + 1))
            sp.wait_ge(z_out[1], 16 * (CHUNKS // 2))

            def load_z(it, c):
                if isinstance(it, int) and it == 0 and c == 2:
                    sp.wait_ge(z_counted, GROUPS)
                wait(sp, elu_ready, (it - 1) * PU + -(-(c * H + H) // 2))
                sp.dma_start(zi_buf[:, c * H:(c + 1) * H, :].rearrange("p a b -> p (a b)"),
                             z_dram[ds(it * CU + c, 1), :, :].rearrange("n p f -> (n p) f")).then_inc(z_in[c], 16)

            def turn_c(it, groups):
                for c in range(groups // H):
                    load_z(it, c)

            sp.wait_ge(flag_ready, 1)
            wide = sp.value_load(flag[0:1, 0:1], min_val=0, max_val=N)
            with sp.If(wide < WIN):
                edge_turns(sp, turn_c)
                sp.wait_ge(elu_ready, (TURNS - 1) * PU + -(-(SHORT + 1) // 2))
                sp.dma_start(zi_buf[:, SHORT, 0:TAIL_E], z_dram[CHUNKS, :, 0:TAIL_E]).then_inc(z_in[SHORT // H], 16)
            with sp.Else():
                sp.wait_ge(z_counted, GROUPS)
                with sp.Fori(0, CHUNKS) as n:
                    for s in range(H):
                        sp.wait_ge(slow_elu, n * H + s + 1)
                        sp.dma_start(e_buf[:, 0, :], z_dram[ds(n, 1), :, s * GE:(s + 1) * GE].rearrange("n p f -> (n p) f")).then_inc(slow_in, 16)
                sp.wait_ge(slow_elu, FULL + 1)
                sp.dma_start(e_buf[:, 0, 0:TAIL_E], z_dram[CHUNKS, :, 0:TAIL_E]).then_inc(slow_in, 16)

            def store_res(it, s):
                wait(sp, res_ready, it * U3 + s + 1)
                sp.dma_start(out_full[:, ds(it * U3 + s, 1), :, :].rearrange("p n t c -> p (n t) c"),
                             z_buf[:, 2 + s, :].rearrange("p (t c) -> p t c", c=C)).then_inc(res_out[s], 16)

            with sp.Fori(0, TURNS3) as it:
                for s in range(U3):
                    store_res(it, s)
            sp.wait_ge(res_ready, CHF + 1)
            sp.dma_start(out[CHF * CH:N, :], z_buf[0:CH_TAIL, 2, 0:C]).then_inc(res_out[0], 16)
            sp.wait_ge(res_out[0], 16 * (TURNS3 + 1))
            sp.wait_ge(res_out[1], 16 * TURNS3)

        @block.gpsimd
        def _(pool):
            pool.memset(x_sb[:, NT - 1, :], 0.0).then_inc(x_cleared, 1)
            pool.memset(dst_raw[:, BLK - 1, :], 0).then_inc(idx_cleared, 1)
            pool.memset(src_raw[:, BLK - 1, :], 0).then_inc(idx_cleared, 1)
            pool.memset(ident[:, :], 0.0).then_inc(ident_zero, 1)
            pool.memset(ones_bf[:, :], 1.0).then_inc(consts_ready, 1)
            for const, value in ((minus_half, -0.5), (minus_one, -1.0), (ln_eps, LN_EPS)):
                pool.memset(const[:, :], value).then_inc(consts_ready, 1)
            pool.iota(iota[:, :], [[1, SWIN]], base=0, channel_multiplier=0,
                      allow_small_or_imprecise_dtypes=True).then_inc(consts_ready, 1)
            pool.wait_ge(ident_zero, 1)
            pool.affine_select(out=ident[:, :], in_=ident[:, :], compare_op=ALU.not_equal, fill=1.0,
                               base=0, pattern=[[-1, P]], channel_multiplier=1).then_inc(consts_ready, 1)
            pool.wait_ge(consts_ready, 6)
            pool.wait_ge(src_in, 64)
            pool.tensor_copy(src_f, src_raw).then_inc(idx_float, 1)
            def turn_a(it):
                pool.wait_ge(ln_step, (it + 1) * LT)
                wait(pool, h_ready, it)
                pool.tensor_tensor(rstd[:, :], ln_mv[:, :, 1], ln_eps[:, :], ALU.add).then_inc(ln_root, 1)
                pool.wait_ge(ln_root, 3 * it + 1)
                pool.tensor_tensor(rstd[:, :], rstd[:, :], minus_half[:, :], ALU.pow).then_inc(ln_root, 1)
                pool.wait_ge(ln_root, 3 * it + 2)
                pool.tensor_tensor(ln_bias[:, :], ln_mv[:, :, 0], rstd[:, :], ALU.mult).then_inc(ln_root, 1)
                pool.wait_ge(ln_root, 3 * it + 3)
                pool.tensor_tensor(ln_bias[:, :], ln_bias[:, :], minus_one[:, :], ALU.mult).then_inc(ln_ready, 1)
                pool.wait_ge(hT_copied, it + 1)
                pool.tensor_copy(hT[:, ds(it * LT * P, LT * P)], hT_st).then_inc(hT_saved, 1)
            node_turns(pool, turn_a)

            def take_indices(it, c, n):
                for s in range(c * H, c * H + H):
                    wait(pool, g_in[s], 16 * K * it)
                pool.tensor_copy(idx_now[:, c * H:c * H + n, :], src_idx[:, ds(count(it, c * H), n), :]).then_inc(idx_copied, 1)

            def gather(s, rows):
                for k in range(K):
                    pool.indirect_dma_start(
                        out=g_buf[0:rows, s, k * C:(k + 1) * C], out_offset=None,
                        in_=p_dram[:, :],
                        in_offset=bass.IndirectOffsetOnAxis(ap=idx_now[0:rows, s, k:k + 1].bitcast(U32), axis=0),
                    ).then_inc(g_in[s], 16)

            def turn_b(it, groups):
                for c in range(groups // H):
                    pool.wait_ge(idx_copied, it * CU + c + 1)
                    wait(pool, z_ready, count(it - 1, c * H + H))
                    if isinstance(it, int) and it == TURNS and c == groups // H - 1:
                        take_indices(TURNS, c + 1, 1)
                    else:
                        take_indices(*norm(it, c + 1, CU), H)
                    for s in range(c * H, c * H + H):
                        gather(s, P)

            take_indices(0, 0, H)
            pool.wait_ge(p_out, 16 * LTURNS)
            edge_turns(pool, turn_b)
            pool.wait_ge(idx_copied, CHUNKS + 1)
            pool.wait_ge(z_ready, count(TURNS - 1, SHORT + 1))
            gather(SHORT, TAIL_ROWS)
            pool.wait_ge(idx_kept, 3 * BLK)
            pool.memset(agg[:, 0, :], 0.0).then_inc(table_cleared, 1)

            pool.wait_ge(bn_step, 1)
            pool.tensor_scalar(bn_k[:, 0:1], bn_mv[:, 1:2], BN_EPS, None, ALU.add).then_inc(bn_root, 1)
            pool.wait_ge(bn_root, 1)
            pool.tensor_tensor(bn_k[:, 0:1], bn_k[:, 0:1], minus_half[:, 0:1], ALU.pow).then_inc(bn_root, 1)

            def line(it, q, groups, cols):
                m = it * PU + q
                for c in sorted({2 * q // H, (2 * q + groups - 1) // H}):
                    pool.wait_ge(z_in[c], 16 * (it + 1))
                wait(pool, elu_turned, m - NPS + 1)

            def line_now(it, q, groups, cols):
                f = q % NPS * 2
                pool.tensor_scalar(f_buf[:, f:f + 2, :].rearrange("p a b -> p (a b)")[:, 0:cols],
                                   zi_buf[:, 2 * q:2 * q + 2, :].rearrange("p a b -> p (a b)")[:, 0:cols],
                                   bn_k[:, 1:2], bn_k[:, 4:5], ALU.mult, ALU.add).then_inc(lin_ready, 1)

            def add_window(it, s):
                n = count(it, s)
                base = pool.value_load(base_row[0:1, ds(n, 1)], min_val=0, max_val=N - 1)
                wait(pool, win_copied, it * PU + s // 2 + 1)
                wait(pool, win_added, n)
                table = agg[:, 0, ds(base, WIN)]
                pool.tensor_tensor(table, table, win_sum[:, s // 2 % 2, s % 2, :], ALU.add).then_inc(win_added, 1)

            def turn_c(it, groups):
                for q in range(groups // 2):
                    after, slot = norm(it, q + 2, PU)
                    following = (after, slot, 2, 2 * GE)
                    if isinstance(it, int) and it == TURNS and slot == SHORT // 2:
                        following = (TURNS, slot, 1, TAIL_E)
                    ends = isinstance(it, int) and it == TURNS and slot > SHORT // 2
                    if not ends:
                        line(*following)
                    for s in range(2 * q - 4, 2 * q - 2):
                        before, slot = norm(it, s, U)
                        if exists(before):
                            add_window(before, slot)
                    if not ends:
                        line_now(*following)

            pool.wait_ge(flag_ready, 1)
            pool.wait_ge(base_in, 16)
            pool.wait_ge(bn1_ready, 1)
            wide = pool.value_load(flag[0:1, 0:1], min_val=0, max_val=N)
            with pool.If(wide < WIN):
                pool.wait_ge(z_ready, GROUPS)
                for q in range(2):
                    line(0, q, 2, 2 * GE)
                    line_now(0, q, 2, 2 * GE)
                edge_turns(pool, turn_c)
                for s in range(SHORT - 4, SHORT + 1):
                    add_window(*norm(TURNS, s, U))
                pool.wait_ge(win_added, GROUPS)
                pool.wait_ge(cnt_added, GROUPS + 1)
                pool.engine_nop().then_inc(agg_done, 1)
            with pool.Else():
                pool.wait_ge(slow_added, GROUPS * NWIN + 1)
                pool.engine_nop().then_inc(agg_done, 1)

            pool.wait_ge(bn_step, 6)
            pool.tensor_scalar(bn2_k[:, 0:1], bn2_mv[:, 1:2], BN_EPS, None, ALU.add).then_inc(bn_root, 1)
            pool.wait_ge(bn_root, 3)
            pool.tensor_tensor(bn2_k[:, 0:1], bn2_k[:, 0:1], minus_half[:, 0:1], ALU.pow).then_inc(bn_root, 1)

        @block.tensor
        def _(pe):
            pe.wait_ge(consts_ready, 6)
            pe.wait_ge(w_in, 32)
            for i, w in enumerate((w1_sb, w2_sb)):
                for j in range(2):
                    last = pe.transpose(ps[:, 6, (2 * i + j) * C:(2 * i + j + 1) * C], w[:, j * C:(j + 1) * C], ident[:, :])
            last.then_inc(w_turned, 1)

            n = 0
            for what, ready, value in ((rel_f, rel_ready, BLK), (dst_f, rel_ready, BLK), (src_f, idx_float, 2)):
                pe.wait_ge(ready, value)
                for j in range(BLK):
                    if n == 1:
                        pe.wait_ge(wT_ready, 1)
                    if n >= 2:
                        pe.wait_ge(idx_kept, n - 1)
                    for k in range(K):
                        last = pe.transpose(ps[:, 7 - n % 2, k * P:(k + 1) * P], what[:, j, k:GE:K], ident[:, :])
                    last.then_inc(idx_turned, 1)
                    n += 1
            pe.wait_ge(span_step, 2)
            pe.wait_ge(idx_kept, n)
            pe.transpose(ps[0:1, 6, 0:P], dspan1[:, 0:1], ident[:, :]).then_inc(span_turned, 1)

            tr_bank = ps[:, 0:2, :].rearrange("p a b -> p (a b)")
            p_bank = ps[:, 2:4, :].rearrange("p a b -> p (a b)")
            pe.wait_ge(wT_ready, 1)
            def turn_a(it):
                pe.wait_ge(h_ready, it + 1)
                wait(pe, hT_copied, it)
                for t in range(LT):
                    last = pe.transpose(tr_bank[:, t * P:(t + 1) * P], h_st[:, t * P:(t + 1) * P], ident[:, :])
                last.then_inc(h_turned, 1)
                pe.wait_ge(hT_copied, it + 1)
                wait(pe, p_added, it)
                for t in range(LT):
                    last = pe.matmul(p_bank[:, t * P:(t + 1) * P], hT_st[:, t * P:(t + 1) * P], wT[:, 0, :], start=True, stop=True)
                last.then_inc(p_product, 1)
            node_turns(pe, turn_a)
            pe.wait_ge(p_added, LTURNS)

            def turn_edges(it, s, rows):
                n = count(it, s)
                if s % H == 0:
                    pe.wait_ge(e_in[s // H % 2], 16 * (uses(it, s, EB) + 1))
                wait(pe, eT_ready, n - NPS + 1)
                for k in range(K):
                    last = pe.transpose(edge_bank[s % NPS][:, k * rows:(k + 1) * rows],
                                        e_buf[0:rows, s % EB, k * C:(k + 1) * C], ident[0:rows, 0:rows])
                last.then_inc(e_turned, 1)

            def product(it, s, rows):
                n = count(it, s)
                bank = z_bank[s % NPS]
                pe.wait_ge(eT_ready, n + 1)
                wait(pe, z_saved, n - NPS + 1)
                pe.matmul(bank[:, 0:K * rows], wT[:, 1, :], t_buf[:, s % NPS, 0:K * rows], start=True, stop=False)
                pe.wait_ge(g_in[s], 16 * K * (it + 1))
                for k in range(K):
                    last = pe.matmul(bank[:, k * rows:(k + 1) * rows], g_buf[0:rows, s, k * C:(k + 1) * C],
                                     ident[0:rows, 0:rows], start=False, stop=(k == K - 1))
                last.then_inc(z_ready, 1)

            def window_counts(it, s, rows):
                n = count(it, s)
                pe.wait_ge(cnt_hot, n + 1)
                wait(pe, cnt_added, n)
                for k in range(K):
                    last = pe.matmul(win_bank[s % 2][:, 0:WIN], ones_bf[0:rows, :], hot_bf[0:rows, s % NPS, k, :],
                                     start=(k == 0), stop=(k == K - 1))
                last.then_inc(cnt_ready, 1)

            def turn_b(it, groups):
                for s in range(groups):
                    if isinstance(it, int) and it == TURNS and s == groups - 1:
                        turn_edges(*TAIL, TAIL_ROWS)
                    else:
                        turn_edges(*norm(it, s + 1, U), P)
                    window_counts(it, s, P)
                    product(it, s, P)

            turn_edges(0, 0, P)
            edge_turns(pe, turn_b)
            window_counts(*TAIL, TAIL_ROWS)
            product(*TAIL, TAIL_ROWS)
            pe.wait_ge(z_saved, GROUPS)
            pe.wait_ge(cnt_added, GROUPS + 1)

            pair_bank = [ps[:, 2 * b:2 * b + 2, :] for b in range(2)]

            def turn_elu(it, q, groups, rows):
                m = it * PU + q
                f = q % NPS * 2
                pe.wait_ge(elu_ready, m + 1)
                wait(pe, elu_edges, m - 2 + 1)
                for g in range(groups):
                    for k in range(K):
                        last = pe.transpose(pair_bank[q % 2][0:rows, g, k * C:(k + 1) * C],
                                            f_buf[:, f + g, k * rows:(k + 1) * rows], ident[:, :])
                last.then_inc(elu_turned, 1)

            def windows(it, q, groups, rows):
                m = it * PU + q
                pe.wait_ge(elu_edges, m + 1)
                pe.wait_ge(hot_ready, m + 1)
                wait(pe, win_copied, m - 2 + 1)
                for g in range(groups):
                    for k in range(K):
                        last = pe.matmul(ps[:, 4 + q % 2 * 2 + g, 0:WARM], m_buf[0:rows, q % NPS * 2 + g, k * C:(k + 1) * C],
                                         one_hot[0:rows, q % NPS, g, k, :], start=(k == 0), stop=(k == K - 1))
                last.then_inc(win_ready, 1)

            def turn_c(it, groups):
                for q in range(groups // 2):
                    turn_elu(it, q, 2, P)
                    before, slot = norm(it, q - 1, PU)
                    if exists(before):
                        windows(before, slot, 2, P)

            pe.wait_ge(flag_ready, 1)
            wide = pe.value_load(flag[0:1, 0:1], min_val=0, max_val=N)
            with pe.If(wide < WIN):
                edge_turns(pe, turn_c)
                turn_elu(TURNS, SHORT // 2, 1, TAIL_ROWS)
                windows(TURNS, SHORT // 2 - 1, 2, P)
                windows(TURNS, SHORT // 2, 1, TAIL_ROWS)
            with pe.Else():
                def slow_group(n, rows):
                    pe.wait_ge(slow_elu, n + 2)
                    for k in range(K):
                        last = pe.transpose(edge_bank[0][0:rows, k * C:(k + 1) * C],
                                            z_buf[:, 0, k * rows:(k + 1) * rows], ident[:, :])
                    last.then_inc(slow_turned, 1)
                    with pe.Fori(0, NWIN) as w:
                        pe.wait_ge(slow_edges, n + 1)
                        step = n * NWIN + w
                        pe.wait_ge(slow_hot, step + 1)
                        pe.wait_ge(slow_added, step + 1)
                        hot = z_buf[0:rows, 2:2 + K, :]
                        for k in range(K):
                            pe.matmul(win_bank[0][:, :], g_buf[0:rows, 0, k * C:(k + 1) * C], hot[:, k, :],
                                      start=(k == 0), stop=(k == K - 1))
                        for k in range(K):
                            last = pe.matmul(win_bank[1][:, :], ones_bf[0:rows, :], hot[:, k, :].bitcast(BF16)[:, 1:2 * SWIN:2],
                                             start=(k == 0), stop=(k == K - 1))
                        last.then_inc(slow_win, 1)
                with pe.Fori(0, FULL) as n:
                    slow_group(n, P)
                slow_group(FULL, TAIL_ROWS)

            def node_product(it, s, cols):
                n = it * U3 + s
                pe.wait_ge(mean_ready, n + 1)
                wait(pe, y_kept, n - 1)
                cs = ds(n * CH, cols)
                pe.matmul(edge_bank[s][:, 0:cols], wT[:, 2, :], hT[:, cs], start=True, stop=False)
                pe.matmul(edge_bank[s][:, 0:cols], wT[:, 3, :], t_buf[:, s, 0:cols], start=False, stop=True).then_inc(y_ready, 1)

            def turn_nodes(it, s, cols):
                n = it * U3 + s
                pe.wait_ge(yelu_ready, n + 1)
                wait(pe, res_ready, n - 1)
                for t in range(-(-cols // P)):
                    rows = min(P, cols - t * P)
                    last = pe.transpose(z_bank[s][0:rows, t * C:(t + 1) * C], g_buf[:, 2 + s, t * P:t * P + rows], ident[:, :])
                last.then_inc(yelu_turned, 1)

            for step in (node_product, turn_nodes):
                for s in range(U3):
                    step(0, s, CH)
                with pe.Fori(1, TURNS3) as it:
                    for s in range(U3):
                        step(it, s, CH)
                step(TURNS3, 0, CH_TAIL)

        @block.scalar
        def _(act):
            for n in range(3 * BLK):
                what, j = n // BLK, n % BLK
                kept = (rel_dst, abs_dst, src_idx)[what]
                act.wait_ge(idx_turned, n + 1)
                size = min(P, GROUPS - j * P)
                act.activation(kept[:, j * P:j * P + size, :].rearrange("p g k -> p k g"),
                               ps[:, 7 - n % 2, :].rearrange("p (k g) -> p k g", k=K)[:, :, 0:size], ACT.Copy).then_inc(idx_kept, 1)
            def turn_a(it):
                act.wait_ge(ln_ready, it + 1)
                wait(act, h_turned, it)
                for t in range(LT):
                    last = act.activation(h_st[:, t * P:(t + 1) * P], x_sb[:, ds(it * LT + t, 1), :].rearrange("p n c -> p (n c)"),
                                          ACT.Relu, bias=ln_bias[:, t:t + 1], scale=rstd[:, t:t + 1])
                last.then_inc(h_ready, 1)

            node_turns(act, turn_a)

            def keep_eT(it, s, rows):
                n = count(it, s)
                act.wait_ge(e_turned, n + 1)
                wait(act, z_ready, n - NPS + 1)
                act.activation(t_buf[:, s % NPS, 0:K * rows], edge_bank[s % NPS][:, 0:K * rows], ACT.Copy).then_inc(eT_ready, 1)

            def keep_z(it, s, rows):
                n = count(it, s)
                act.wait_ge(z_ready, n + 1)
                if s % H == 0:
                    wait(act, z_out[s // H % 2], 16 * uses(it, s, EB))
                wait(act, z_counted, n - EB + 1)
                act.activation(z_buf[:, s % EB, 0:K * rows], z_bank[s % NPS][:, 0:K * rows], ACT.Copy).then_inc(z_saved, 1)

            def turn_b(it, groups):
                for s in range(groups):
                    keep_eT(it, s, P)
                    before, slot = norm(it, s - 1, U)
                    if exists(before):
                        keep_z(before, slot, P)

            edge_turns(act, turn_b)
            keep_eT(*TAIL, TAIL_ROWS)
            keep_z(TURNS, SHORT - 1, P)
            keep_z(*TAIL, TAIL_ROWS)

            def exponent(it, q, groups, cols):
                m = it * PU + q
                for c in sorted({2 * q // H, (2 * q + groups - 1) // H}):
                    act.wait_ge(z_in[c], 16 * (it + 1))
                wait(act, elu_ready, m - 2 + 1)
                x = q % 2 * 2
                act.activation(x_buf[:, x:x + 2, :].rearrange("p a b -> p (a b)")[:, 0:cols],
                               zi_buf[:, 2 * q:2 * q + 2, :].rearrange("p a b -> p (a b)")[:, 0:cols], ACT.Exp,
                               bias=bn_k[:, 3:4], scale=bn_k[:, 1:2]).then_inc(exp_ready, 1)

            def keep_elu(it, q, groups, rows):
                m = it * PU + q
                act.wait_ge(elu_turned, m + 1)
                wait(act, win_ready, m - NPS + 1)
                f = q % NPS * 2
                b = q % 2 * 2
                act.activation(m_buf[0:rows, f:f + groups, :], ps[0:rows, b:b + groups, :], ACT.Copy).then_inc(elu_edges, 1)

            def turn_c(it, groups):
                for q in range(groups // 2):
                    exponent(it, q, 2, 2 * GE)
                    before, slot = norm(it, q - 1, PU)
                    if exists(before):
                        keep_elu(before, slot, 2, P)

            act.wait_ge(flag_ready, 1)
            wide = act.value_load(flag[0:1, 0:1], min_val=0, max_val=N)
            act.wait_ge(bn1_ready, 1)
            with act.If(wide < WIN):
                act.wait_ge(z_ready, GROUPS)
                edge_turns(act, turn_c)
                exponent(TURNS, SHORT // 2, 1, TAIL_E)
                keep_elu(TURNS, SHORT // 2 - 1, 2, P)
                keep_elu(TURNS, SHORT // 2, 1, TAIL_ROWS)
            with act.Else():
                def slow_group(n, rows):
                    act.wait_ge(slow_in, 16 * (n + 1))
                    act.activation(t_buf[:, 0, 0:K * rows], e_buf[:, 0, 0:K * rows], ACT.Exp,
                                   bias=bn_k[:, 3:4], scale=bn_k[:, 1:2]).then_inc(slow_exp, 1)
                    act.wait_ge(slow_turned, n + 2)
                    act.wait_ge(slow_win, n * NWIN + 1)
                    act.activation(g_buf[0:rows, 0, :], edge_bank[0][0:rows, :], ACT.Copy).then_inc(slow_edges, 1)
                with act.Fori(0, FULL) as n:
                    slow_group(n, P)
                slow_group(FULL, TAIL_ROWS)

            def keep_y(it, s, cols):
                n = it * U3 + s
                act.wait_ge(y_ready, n + 1)
                act.activation(hT[:, ds(n * CH, cols)], edge_bank[s][:, 0:cols], ACT.Identity, bias=vecs[:, 2:3]).then_inc(y_kept, 1)

            def node_exponent(it, s, cols):
                n = it * U3 + s
                wait(act, yelu_ready, n - 1)
                act.activation(t_buf[:, s, 0:cols], hT[:, ds(n * CH, cols)], ACT.Exp,
                               bias=bn2_k[:, 3:4], scale=bn2_k[:, 1:2]).then_inc(yexp_ready, 1)

            for step in (keep_y, node_exponent):
                if step is node_exponent:
                    act.wait_ge(bn2_ready, 1)
                for s in range(U3):
                    step(0, s, CH)
                with act.Fori(1, TURNS3) as it:
                    for s in range(U3):
                        step(it, s, CH)
                step(TURNS3, 0, CH_TAIL)

        @block.vector
        def _(dve):
            dve.wait_ge(dst_in, 64)
            dve.tensor_copy(dst_f, dst_raw).then_inc(idx_float, 1)
            dve.wait_ge(idx_float, 1)
            dve.wait_ge(idx_float, 2)
            dve.tensor_reduce(dmin[:, :], dst_f, AX_X, ALU.min).then_inc(dminmax, 1)
            dve.tensor_reduce(dmax[:, :], dst_f, AX_X, ALU.max).then_inc(dminmax, 1)
            dve.wait_ge(dminmax, 2)
            for j in range(BLK):
                dve.tensor_scalar(rel_f[:, j, :], dst_f[:, j, :], dmin[:, j:j + 1], None, ALU.subtract).then_inc(rel_ready, 1)
            dve.tensor_copy(base_i[:, :], dmin[:, :]).then_inc(base_ready, 1)
            dve.tensor_tensor(dspan[:, :], dmax[:, :], dmin[:, :], ALU.subtract).then_inc(span_step, 1)
            dve.wait_ge(span_step, 1)
            dve.tensor_reduce(dspan1[:, :], dspan[:, :], AX_X, ALU.max).then_inc(span_step, 1)
            dve.wait_ge(w_turned, 1)
            dve.tensor_copy(wT[:, :, :].rearrange("p a b -> p (a b)"), ps[:, 6, :]).then_inc(wT_ready, 1)
            dve.wait_ge(x_first, 16)
            tr_bank = ps[:, 0:2, :].rearrange("p a b -> p (a b)")
            p_bank = ps[:, 2:4, :].rearrange("p a b -> p (a b)")
            def layer_statistics(it):
                wait(dve, ln_ready, it)
                for t in range(LT):
                    dve.bn_stats(ln_st[:, t, :], x_sb[:, ds(it * LT + t, 1), :].rearrange("p n c -> p (n c)"))
                dve.drain()
                for t in range(LT):
                    dve.bn_aggr(ln_mv[:, t, :], ln_st[:, t, :]).then_inc(ln_step, 1)

            def node_table(it):
                dve.wait_ge(h_turned, it + 1)
                wait(dve, hT_saved, it)
                wait(dve, p_product, it)
                dve.tensor_copy(hT_st, tr_bank[:, 0:LT * P]).then_inc(hT_copied, 1)
                dve.wait_ge(p_product, it + 1)
                wait(dve, p_out, 16 * it)
                dve.tensor_tensor(p_st.rearrange("p (t c) -> p t c", c=C), p_bank[:, 0:LT * P].rearrange("p (t c) -> p t c", c=C),
                                  b1_rows[:, :].unsqueeze(1).to_broadcast([P, LT, C]), ALU.add).then_inc(p_added, 1)

            def turn_a(it):
                layer_statistics(it + 1)
                node_table(it)

            layer_statistics(0)
            dve.wait_ge(vec_in, 16 * 6)
            dve.wait_ge(x_in, 32)
            node_turns(dve, turn_a, last=LTURNS - 1)
            node_table(LTURNS - 1)
            dve.wait_ge(span_turned, 1)
            dve.tensor_reduce(span_all[:, :], ps[0:1, 6, 0:P], AX_X, ALU.max).then_inc(span_step, 1)
            dve.wait_ge(span_step, 3)
            dve.tensor_copy(flag[:, :], span_all[:, :]).then_inc(flag_ready, 1)

            dve.wait_ge(idx_kept, 3 * BLK)
            dve.memset(agg[:, 1, :], 0.0).then_inc(cnt_added, 1)
            dve.wait_ge(base_in, 16)

            def statistics(it, s, rows):
                n = count(it, s)
                dve.wait_ge(z_saved, n + 1)
                dve.bn_stats(stats[:, ds(n, 1), :].rearrange("p n f -> p (n f)"), z_buf[:, s % EB, 0:K * rows]).then_inc(z_counted, 1)

            def hot(matrix, n, groups, rows):
                return dve.tensor_tensor(
                    matrix,
                    rel_dst[0:rows, ds(n, groups), :].rearrange("p n k -> p (n k)").unsqueeze(2).to_broadcast([rows, groups * K, WIN]),
                    iota[0:rows, 0:WIN].unsqueeze(1).to_broadcast([rows, groups * K, WIN]),
                    ALU.is_equal)

            def count_hot(it, s, rows):
                n = count(it, s)
                wait(dve, cnt_ready, n - NPS + 1)
                hot(hot_bf[0:rows, s % NPS, :, :], n, 1, rows).then_inc(cnt_hot, 1)

            def add_counts(it, s):
                n = count(it, s)
                base = dve.value_load(base_row[0:1, ds(n, 1)], min_val=0, max_val=N - 1)
                dve.wait_ge(cnt_ready, n + 1)
                dve.wait_ge(cnt_added, n + 1)
                table = agg[:, 1, ds(base, WIN)]
                dve.tensor_tensor(table, table, win_bank[s % 2][:, 0:WIN], ALU.add).then_inc(cnt_added, 1)

            def turn_b(it, groups):
                for s in range(groups):
                    count_hot(it, s, P)
                    before, slot = norm(it, s - 1, U)
                    if exists(before):
                        add_counts(before, slot)
                        statistics(before, slot, P)

            edge_turns(dve, turn_b)
            count_hot(*TAIL, TAIL_ROWS)
            add_counts(TURNS, SHORT - 1)
            statistics(TURNS, SHORT - 1, P)
            add_counts(*TAIL)
            statistics(*TAIL, TAIL_ROWS)

            def bn_constants(mv, k, weight, bias, first, root):
                dve.wait_ge(bn_root, root)
                dve.tensor_tensor(k[:, 1:2], k[:, 0:1], weight, ALU.mult).then_inc(bn_step, 1)
                dve.wait_ge(bn_step, first + 1)
                dve.tensor_tensor(k[:, 2:3], mv[:, 0:1], k[:, 1:2], ALU.mult).then_inc(bn_step, 1)
                dve.wait_ge(bn_step, first + 2)
                dve.tensor_tensor(k[:, 3:4], bias, k[:, 2:3], ALU.subtract).then_inc(bn_step, 1)
                dve.wait_ge(bn_step, first + 3)
                dve.tensor_scalar(k[:, 4:5], k[:, 3:4], 1.0, None, ALU.add).then_inc(bn_step, 1)
                dve.wait_ge(bn_step, first + 4)

            dve.wait_ge(z_counted, GROUPS)
            dve.bn_aggr(bn_mv[:, :], stats[:, :, :].rearrange("p n f -> p (n f)")).then_inc(bn_step, 1)
            bn_constants(bn_mv, bn_k, vecs[:, 0:1], vecs[:, 1:2], 1, 2)
            dve.engine_nop().then_inc(bn1_ready, 1)

            def elu(it, q, cols):
                m = it * PU + q
                f = q % NPS * 2
                x = q % 2 * 2
                line = f_buf[:, f:f + 2, :].rearrange("p a b -> p (a b)")[:, 0:cols]
                dve.wait_ge(lin_ready, m + 1)
                dve.wait_ge(exp_ready, m + 1)
                dve.scalar_tensor_tensor(out=line, in0=x_buf[:, x:x + 2, :].rearrange("p a b -> p (a b)")[:, 0:cols],
                                         scalar=1.0, in1=line, op0=ALU.min, op1=ALU.max).then_inc(elu_ready, 1)

            def sum_hot(it, q, groups, rows):
                m = it * PU + q
                wait(dve, win_ready, m - NPS + 1)
                hot(one_hot[0:rows, q % NPS, 0:groups, :, 0:WIN].rearrange("p g k w -> p (g k) w"),
                    count(it, 2 * q), groups, rows).then_inc(hot_ready, 1)

            def copy_windows(it, q, groups):
                m = it * PU + q
                dve.wait_ge(win_ready, m + 1)
                wait(dve, win_added, 2 * (m - 1))
                b = 4 + q % 2 * 2
                dve.tensor_copy(win_sum[:, q % 2, 0:groups, :], ps[:, b:b + groups, 0:WIN]).then_inc(win_copied, 1)

            def turn_c(it, groups):
                for q in range(groups // 2):
                    elu(it, q, 2 * GE)
                    before, slot = norm(it, q - 2, PU)
                    if exists(before):
                        copy_windows(before, slot, 2)
                    sum_hot(it, q, 2, P)

            dve.memset(one_hot[:, :, :, :, :].rearrange("p n g k w -> p (n g k w)"), 0.0).then_inc(hot_cleared, 1)
            dve.wait_ge(hot_cleared, 1)
            dve.wait_ge(table_cleared, 1)
            wide = dve.value_load(flag[0:1, 0:1], min_val=0, max_val=N)
            with dve.If(wide < WIN):
                edge_turns(dve, turn_c)
                elu(TURNS, SHORT // 2, TAIL_E)
                copy_windows(TURNS, SHORT // 2 - 2, 2)
                sum_hot(TURNS, SHORT // 2, 1, TAIL_ROWS)
                copy_windows(TURNS, SHORT // 2 - 1, 2)
                copy_windows(TURNS, SHORT // 2, 1)
            with dve.Else():
                for ahead in (slow_elu, slow_turned, slow_win):
                    dve.engine_nop().then_inc(ahead, 1)
                dve.wait_ge(cnt_added, GROUPS + 1)
                dve.memset(agg[:, 1, :], 0.0).then_inc(slow_added, 1)
                dve.wait_ge(slow_added, 1)

                def slow_group(n, rows):
                    line = z_buf[:, 0, 0:K * rows]
                    now = one_hot[:, 0, 0, 0, 0:K]
                    dve.wait_ge(slow_in, 16 * (n + 1))
                    dve.wait_ge(slow_turned, n + 1)
                    dve.tensor_scalar(line, e_buf[:, 0, 0:K * rows], bn_k[:, 1:2], bn_k[:, 4:5], ALU.mult, ALU.add).then_inc(slow_lin, 1)
                    dve.wait_ge(slow_lin, n + 1)
                    dve.wait_ge(slow_exp, n + 1)
                    dve.scalar_tensor_tensor(out=line, in0=t_buf[:, 0, 0:K * rows], scalar=1.0, in1=line,
                                             op0=ALU.min, op1=ALU.max).then_inc(slow_elu, 1)
                    dve.tensor_copy(now, abs_dst[:, ds(n, 1), :].rearrange("p n k -> p (n k)")).then_inc(slow_dst, 1)
                    with dve.Fori(0, NWIN) as w:
                        step = n * NWIN + w
                        dve.wait_ge(slow_dst, n * (NWIN + 1) + w + 1)
                        dve.wait_ge(slow_win, step + 1)
                        for k in range(K):
                            last = dve.tensor_scalar(z_buf[:, 2 + k, :], iota[:, :], now[:, k:k + 1], None, ALU.is_equal)
                        last.then_inc(slow_hot, 1)
                        dve.wait_ge(slow_hot, step + 1)
                        dve.tensor_scalar(now, now, float(SWIN), None, ALU.subtract).then_inc(slow_dst, 1)
                        dve.wait_ge(slow_win, step + 2)
                        table = agg[:, :, ds(w * SWIN, SWIN)]
                        dve.tensor_tensor(table, table, ps[:, 6:8, :], ALU.add).then_inc(slow_added, 1)
                        dve.wait_ge(slow_added, step + 2)
                with dve.Fori(0, FULL) as n:
                    slow_group(n, P)
                slow_group(FULL, TAIL_ROWS)

            def mean(it, s, cols):
                n = it * U3 + s
                cs = ds(n * CH, cols)
                cnt = z_buf[:, s, 0:cols]
                dif = z_buf[:, 4 + s, 0:cols]
                wait(dve, y_ready, n - 1)
                dve.tensor_scalar(cnt, agg[:, 1, cs], 1.0, None, ALU.max).then_inc(mean_step, 1)
                dve.tensor_tensor(dif, agg[:, 0, cs], agg[:, 1, cs], ALU.subtract).then_inc(mean_step, 1)
                dve.wait_ge(mean_step, 3 * n + 2)
                dve.reciprocal(cnt, cnt).then_inc(mean_step, 1)
                dve.wait_ge(mean_step, 3 * n + 3)
                dve.tensor_tensor(t_buf[:, s, 0:cols], dif, cnt, ALU.mult).then_inc(mean_ready, 1)

            def node_statistics(it, s, cols):
                n = it * U3 + s
                dve.wait_ge(y_kept, n + 1)
                dve.bn_stats(stats2[:, ds(n, 1), :].rearrange("p n f -> p (n f)"), hT[:, ds(n * CH, cols)]).then_inc(y_counted, 1)

            def node_elu(it, s, cols):
                n = it * U3 + s
                line = g_buf[:, 2 + s, 0:cols]
                wait(dve, yelu_turned, n - 1)
                dve.tensor_scalar(line, hT[:, ds(n * CH, cols)], bn2_k[:, 1:2], bn2_k[:, 4:5], ALU.mult, ALU.add).then_inc(ylin_ready, 1)
                dve.wait_ge(ylin_ready, n + 1)
                dve.wait_ge(yexp_ready, n + 1)
                dve.scalar_tensor_tensor(out=line, in0=t_buf[:, s, 0:cols], scalar=1.0, in1=line,
                                         op0=ALU.min, op1=ALU.max).then_inc(yelu_ready, 1)

            def residual(it, s, cols):
                n = it * U3 + s
                tiles = -(-cols // P)
                rows = min(P, cols)
                dve.wait_ge(yelu_turned, n + 1)
                wait(dve, res_out[s], 16 * it)
                dve.scalar_tensor_tensor(out=z_buf[0:rows, 2 + s, 0:tiles * C], in0=z_bank[s][0:rows, 0:tiles * C], scalar=-1.0,
                                         in1=x_sb[0:rows, ds(n * (CH // P), tiles), :].rearrange("p t c -> p (t c)"),
                                         op0=ALU.add, op1=ALU.add).then_inc(res_ready, 1)

            dve.wait_ge(agg_done, 1)
            for first, second in ((mean, node_statistics), (node_elu, residual)):
                first(0, 0, CH)
                first(0, 1, CH)
                second(0, 0, CH)
                with dve.Fori(1, TURNS3) as it:
                    first(it, 0, CH)
                    second(it - 1, 1, CH)
                    first(it, 1, CH)
                    second(it, 0, CH)
                first(TURNS3, 0, CH_TAIL)
                second(TURNS3 - 1, 1, CH)
                second(TURNS3, 0, CH_TAIL)
                if first is mean:
                    dve.wait_ge(y_counted, CHF + 1)
                    dve.bn_aggr(bn2_mv[:, :], stats2[:, :, :].rearrange("p n f -> p (n f)")).then_inc(bn_step, 1)
                    bn_constants(bn2_mv, bn2_k, vecs[:, 3:4], vecs[:, 4:5], 6, 4)
                    dve.engine_nop().then_inc(bn2_ready, 1)


_INS = ["x", "src", "dst", "edge_attr_128", "L0_gnn_w1", "L0_gnn_b1", "L0_gnn_bn1_w", "L0_gnn_bn1_b",
        "L0_gnn_w2", "L0_gnn_b2", "L0_gnn_bn2_w", "L0_gnn_bn2_b"]


def kernel(**inputs):
    import numpy as _np
    import concourse.bacc as _bacc
    from concourse import mybir as _mybir
    from concourse.bass_utils import run_bass_kernel_spmd as _run

    nc = _bacc.Bacc("TRN2", target_bir_lowering=False, num_devices=1)
    arrays, args = {}, []
    for name in _INS:
        a = _np.ascontiguousarray(inputs[name])
        arrays[f"in_{name}"] = a
        args.append(nc.dram_tensor(f"in_{name}", a.shape, _mybir.dt.from_np(a.dtype), kind="ExternalInput").ap())
    shape = inputs["x"].shape
    args.append(nc.dram_tensor("out_0", shape, _mybir.dt.float32, kind="ExternalOutput").ap())
    gnn_kernel(nc, *args)
    r = _run(nc, [arrays], core_ids=[0])
    return r.results[0]["out_0"]
```

```python
from contextlib import ExitStack

import concourse.bass as bass
from concourse import mybir

F32 = mybir.dt.float32
BF16 = mybir.dt.bfloat16
I32 = mybir.dt.int32
U32 = mybir.dt.uint32
ALU = mybir.AluOpType
ACT = mybir.ActivationFunctionType
AX_X = mybir.AxisListType.X
ds = bass.ds

P = 128
K = 4
GE = P * K
U = 12
H = 3
CU = U // H
EB = 6
NPS = 3
PU = U // 2
WIN = 48
HALF = 64
BANK = 512
LN_EPS = 1e-5
BN_EPS = 1e-5
LT = 7


def wait(eng, sem, value):
    if isinstance(value, int) and value <= 0:
        return
    eng.wait_ge(sem, value)


def norm(it, s, unroll):
    return it + s // unroll, s % unroll


def exists(it):
    return not (isinstance(it, int) and it < 0)


def gnn_kernel(nc, x, src, dst, edge_attr, w1, b1, bn1_w, bn1_b, w2, b2, bn2_w, bn2_b, out):
    N, C = x.shape
    E = edge_attr.shape[0]
    assert C == P
    NT = -(-N // P)
    NP = NT * P
    N_LAST = N - (NT - 1) * P
    LTURNS = NT // LT
    assert LTURNS * LT == NT
    FULL = E // GE
    TURNS = FULL // U
    SHORT = FULL - TURNS * U
    assert TURNS >= 3 and SHORT == EB and FULL % H == 0
    TAIL_ROWS = (E - FULL * GE) // K
    assert 0 < TAIL_ROWS < P and FULL * GE + TAIL_ROWS * K == E
    GROUPS = FULL + 1
    BLK = -(-GROUPS // P)
    B_ROWS = FULL - (BLK - 1) * P
    TAIL_E = TAIL_ROWS * K
    TAIL = (TURNS, SHORT)
    CHUNKS = FULL // H
    SWIN = BANK
    NWIN = -(-N // SWIN)
    TABLE = max(NWIN * SWIN, N + WIN)
    PARTS = TURNS - 1
    COLS = -(-N // PARTS)
    assert PARTS <= P and PARTS * COLS <= TABLE and 2 * GE + 2 * COLS <= GROUPS * K
    CH = BANK
    CHF = N // CH
    U3 = 4
    TURNS3 = CHF // U3
    assert TURNS3 * U3 == CHF and TURNS3 >= 3
    CH_TAIL = N - CHF * CH
    assert CH_TAIL <= P

    p_dram = nc.dram_tensor("p_table", [NP, C], F32, kind="Internal").ap()
    z_dram = nc.dram_tensor("z_edges", [CHUNKS + 1, P, H * GE], F32, kind="Internal").ap()
    cnt_dram = nc.dram_tensor("counts", [PARTS * COLS], F32, kind="Internal").ap()
    inv_dram = nc.dram_tensor("inverse_counts", [PARTS * COLS], F32, kind="Internal").ap()
    base_dram = nc.dram_tensor("base_row_dram", [BLK * P], I32, kind="Internal").ap()

    with ExitStack() as ctx:
        def sb(name, shape, dt=F32):
            return ctx.enter_context(nc.sbuf_tensor(name, shape, dt))

        def sem(name):
            return ctx.enter_context(nc.semaphore(name))

        ps = ctx.enter_context(nc.psum_tensor("ps", [P, 8, BANK], F32))

        ident = sb("ident", [P, P])
        ones_bf = sb("ones_bf", [P, P], BF16)
        minus_half = sb("minus_half", [P, LT])
        minus_one = sb("minus_one", [P, LT])
        ln_eps = sb("ln_eps", [P, LT])
        iota = sb("iota", [P, SWIN])
        w1_sb = sb("w1_sb", [P, 2 * C])
        w2_sb = sb("w2_sb", [P, 2 * C])
        wT = sb("wT", [P, 4, C])
        b1_rows = sb("b1_rows", [P, C])
        vecs = sb("vecs", [P, 5])
        x_sb = sb("x_sb", [P, NT, C])
        hT = sb("hT", [P, NP])
        agg = sb("agg", [P, 2, TABLE])
        agg_flat = agg[:, :, :].rearrange("p a n -> p (a n)")
        src_idx = sb("src_idx", [P, GROUPS, K], I32)
        rel_dst = sb("rel_dst", [P, GROUPS, K])
        abs_dst = sb("abs_dst", [P, GROUPS, K])
        base_row = sb("base_row", [1, BLK * P], I32)
        flag = sb("flag", [1, 1], I32)
        IB = BLK * GE
        assert 5 * IB <= 2 * TABLE
        raw = [agg_flat[:, i * IB:(i + 1) * IB] for i in range(5)]
        src_raw = raw[0].bitcast(I32).rearrange("p (j e) -> p j e", j=BLK)
        dst_raw = raw[1].bitcast(I32).rearrange("p (j e) -> p j e", j=BLK)
        src_f, dst_f, rel_f = [r.rearrange("p (j e) -> p j e", j=BLK) for r in raw[2:5]]
        dmin = sb("dmin", [P, BLK])
        dmax = sb("dmax", [P, BLK])
        dspan = sb("dspan", [P, BLK])
        dspan1 = sb("dspan1", [P, 1])
        span_all = sb("span_all", [1, 1])
        base_i = sb("base_i", [P, BLK], I32)
        edge_buf = sb("edge_buf", [P, 2 * EB + U + 4, GE])
        e_buf = edge_buf[:, 0:EB, :]
        z_buf = edge_buf[:, EB:2 * EB, :]
        g_buf = edge_buf[:, 2 * EB:2 * EB + U, :]
        t_buf = edge_buf[:, 2 * EB + U:, :]
        zi_buf = edge_buf[:, 0:U, :]
        f_buf = g_buf[:, 0:6, :]
        m_buf = g_buf[:, 6:12, :]
        idx_now = sb("idx_now", [P, U, K], I32)
        hot_bf = sb("hot_bf", [P, NPS, K, WIN], BF16)
        one_hot = sb("one_hot", [P, NPS, 2, K, HALF])
        win_rows = sb("win_rows", [P, 2, C])
        win_sum = sb("win_sum", [P, 2, 2, WIN])
        stats = sb("stats", [P, GROUPS, 6])
        src_space = src_idx[:, :, :].rearrange("p g k -> p (g k)").bitcast(F32)
        x_buf = [t_buf[:, b:b + 2, :].rearrange("p a b -> p (a b)") for b in (0, 2)] + [src_space[:, 0:2 * GE]]
        cnt_part, inv_part = [src_space[0:PARTS, 2 * GE + i * COLS:2 * GE + (i + 1) * COLS] for i in range(2)]
        bn_mv = sb("bn_mv", [P, 2])
        bn_k = sb("bn_k", [P, 5])
        stats2 = sb("stats2", [P, CHF + 1, 6])
        bn2_mv = sb("bn2_mv", [P, 2])
        bn2_k = sb("bn2_k", [P, 5])
        ratio_buf = edge_buf[:, 0:U3, :]
        res_buf = edge_buf[:, U3:2 * U3, :]
        node_buf = g_buf[:, 0:U3, :]
        h_st = e_buf[:, 0:2, :].rearrange("p a b -> p (a b)")[:, 0:LT * P]
        hT_st = e_buf[:, 2:4, :].rearrange("p a b -> p (a b)")[:, 0:LT * P]
        p_st = e_buf[:, 4:6, :].rearrange("p a b -> p (a b)")[:, 0:LT * P]
        ln_st = g_buf[:, 0, 0:NT * 6].rearrange("p (t f) -> p t f", f=6)
        ln_mv = g_buf[:, 1, 0:NT * 2].rearrange("p (t f) -> p t f", f=2)
        rstd, ln_bias = [g_buf[:, 2, i * NT:(i + 1) * NT] for i in range(2)]

        x_cleared = sem("x_cleared")
        x_first = sem("x_first")
        x_second = sem("x_second")
        x_in = sem("x_in")
        w_in = sem("w_in")
        vec_in = sem("vec_in")
        idx_cleared = sem("idx_cleared")
        src_in = sem("src_in")
        dst_in = sem("dst_in")
        ident_zero = sem("ident_zero")
        consts_ready = sem("consts_ready")
        w_turned = sem("w_turned")
        wT_ready = sem("wT_ready")
        idx_float = sem("idx_float")
        dminmax = sem("dminmax")
        rel_ready = sem("rel_ready")
        base_ready = sem("base_ready")
        base_out = sem("base_out")
        base_in = sem("base_in")
        span_step = sem("span_step")
        span_turned = sem("span_turned")
        flag_ready = sem("flag_ready")
        idx_turned = sem("idx_turned")
        idx_kept = sem("idx_kept")
        ln_step = sem("ln_step")
        ln_root = sem("ln_root")
        ln_ready = sem("ln_ready")
        h_ready = sem("h_ready")
        h_turned = sem("h_turned")
        hT_copied = sem("hT_copied")
        hT_saved = sem("hT_saved")
        p_product = sem("p_product")
        p_added = sem("p_added")
        p_out = sem("p_out")
        e_in = [sem(f"e_in{h}") for h in range(2)]
        z_out = [sem(f"z_out{h}") for h in range(2)]
        g_in = [sem(f"g_in{s}") for s in range(U)]
        idx_copied = sem("idx_copied")
        e_turned = sem("e_turned")
        eT_ready = sem("eT_ready")
        z_ready = sem("z_ready")
        z_counted = sem("z_counted")
        z_saved = sem("z_saved")
        bn_step = sem("bn_step")
        bn_root = sem("bn_root")
        bn1_ready = sem("bn1_ready")
        cnt_hot = sem("cnt_hot")
        cnt_ready = sem("cnt_ready")
        cnt_added = sem("cnt_added")
        counts_cleared = sem("counts_cleared")
        z_in = [sem(f"z_in{c}") for c in range(CU)]
        exp_ready = sem("exp_ready")
        lin_ready = sem("lin_ready")
        elu_ready = sem("elu_ready")
        elu_turned = sem("elu_turned")
        elu_edges = sem("elu_edges")
        hot_cleared = sem("hot_cleared")
        hot_ready = sem("hot_ready")
        win_ready = sem("win_ready")
        rows_copied = sem("rows_copied")
        win_turned = sem("win_turned")
        win_copied = sem("win_copied")
        win_added = sem("win_added")
        slow_in = sem("slow_in")
        slow_exp = sem("slow_exp")
        slow_lin = sem("slow_lin")
        slow_elu = sem("slow_elu")
        slow_turned = sem("slow_turned")
        slow_edges = sem("slow_edges")
        slow_dst = sem("slow_dst")
        slow_hot = sem("slow_hot")
        slow_win = sem("slow_win")
        slow_added = sem("slow_added")
        cnt_out = sem("cnt_out")
        cnt_in = sem("cnt_in")
        cnt_step = sem("cnt_step")
        inv_out = sem("inv_out")
        inv_in = sem("inv_in")
        ratio_ready = sem("ratio_ready")
        mean_ready = sem("mean_ready")
        y_ready = sem("y_ready")
        y_kept = sem("y_kept")
        y_counted = sem("y_counted")
        bn2_ready = sem("bn2_ready")
        yexp_ready = sem("yexp_ready")
        ylin_ready = sem("ylin_ready")
        yelu_ready = sem("yelu_ready")
        yelu_turned = sem("yelu_turned")
        res_ready = sem("res_ready")
        res_out = [sem(f"res_out{s}") for s in range(U3)]

        e_full = edge_attr[0:FULL * GE, :].rearrange("(g p k) c -> p g (k c)", p=P, k=K)
        e_tail = edge_attr[FULL * GE:E, :].rearrange("(p k) c -> p (k c)", k=K)
        out_full = out[0:CHF * CH, :].rearrange("(n t p) c -> p n t c", p=P, t=CH // P)

        def count(it, s):
            return it * U + s

        edge_bank = [ps[:, b, :] for b in range(NPS)]
        z_bank = [ps[:, NPS + b, :] for b in range(NPS)]
        win_bank = [ps[:, 6 + b, :] for b in range(2)]

        y_bank = [ps[:, b, :] for b in range(U3)]
        turn_bank = [ps[:, U3 + b, :] for b in range(U3)]

        def uses(it, s, depth):
            return it * (U // depth) + s // depth

        def edge_turns(eng, turn):
            turn(0, U)
            with eng.Fori(1, TURNS) as it:
                turn(it, U)
            turn(TURNS, SHORT)

        def node_turns(eng, turn, first=0, last=LTURNS):
            turn(first)
            with eng.Fori(first + 1, last) as it:
                turn(it)

        def load_indices(eng, raw_idx, ids, landed):
            b0 = (BLK - 1) * P * GE
            eng.dma_start(raw_idx[:, 0:BLK - 1, :], ids[0:b0].rearrange("(j g e) -> g j e", g=P, e=GE)).then_inc(landed, 16)
            eng.dma_start(raw_idx[0:B_ROWS, BLK - 1, :], ids[b0:FULL * GE].rearrange("(g e) -> g e", e=GE)).then_inc(landed, 16)
            eng.dma_start(raw_idx[B_ROWS:B_ROWS + 1, BLK - 1, 0:TAIL_E],
                          ids[FULL * GE:E].rearrange("(g e) -> g e", g=1)).then_inc(landed, 16)
            eng.dma_start(raw_idx[B_ROWS:B_ROWS + 1, BLK - 1, TAIL_E:GE],
                          ids[FULL * GE:FULL * GE + GE - TAIL_E].rearrange("(g e) -> g e", g=1)).then_inc(landed, 16)

        def node_chunks(eng, step):
            for s in range(U3):
                step(0, s, CH)
            with eng.Fori(1, TURNS3) as it:
                for s in range(U3):
                    step(it, s, CH)
            step(TURNS3, 0, CH_TAIL)

        block = ctx.enter_context(nc.Block())

        @block.sync
        def _(sp):
            def load_x(t0, t1, landed):
                sp.dma_start(x_sb[:, t0:t1, :], x[t0 * P:t1 * P, :].rearrange("(t p) c -> p t c", p=P)).then_inc(landed, 16)

            last_x = NT - 1
            load_x(0, LT, x_first)
            sp.wait_ge(idx_cleared, 1)
            load_indices(sp, src_raw, src, src_in)
            load_x(LT, 3 * LT, x_second)
            load_x(3 * LT, last_x, x_in)
            sp.wait_ge(x_cleared, 1)
            sp.dma_start(x_sb[0:N_LAST, last_x, :], x[last_x * P:N, :]).then_inc(x_in, 16)
            sp.wait_ge(idx_cleared, 2)
            load_indices(sp, dst_raw, dst, dst_in)
            for i, v in enumerate((bn1_w, bn1_b, b2, bn2_w, bn2_b)):
                sp.dma_start(vecs[:, i:i + 1], v.rearrange("(c o) -> c o", o=1)).then_inc(vec_in, 16)
            p_view = p_dram.rearrange("(n t p) c -> p n t c", p=P, t=LT)
            def turn_a(it):
                sp.wait_ge(p_added, it + 1)
                sp.dma_start(p_view[:, ds(it, 1), :, :].rearrange("p n t c -> p (n t) c"),
                             p_st.rearrange("p (t c) -> p t c", c=C)).then_inc(p_out, 16)
            node_turns(sp, turn_a)
            sp.wait_ge(p_out, 16 * LTURNS)
            sp.wait_ge(hT_saved, LTURNS)

            def load_edges(it, c):
                n = count(it, c * H)
                half = c % 2
                wait(sp, e_turned, n - EB + H)
                sp.dma_start(e_buf[:, half * H:(half + 1) * H, :], e_full[:, ds(n, H), :]).then_inc(e_in[half], 16)

            def store_z(it, c):
                half = c % 2
                wait(sp, z_saved, count(it, c * H + H))
                sp.dma_start(z_dram[ds(it * CU + c, 1), :, :].rearrange("n p f -> (n p) f"),
                             z_buf[:, half * H:(half + 1) * H, :].rearrange("p a b -> p (a b)")).then_inc(z_out[half], 16)

            def turn_b(it, groups, base_step=False):
                for c in range(groups // H):
                    load_edges(it, c)
                    if base_step and c == 1:
                        sp.wait_ge(base_ready, 1)
                        sp.dma_start(base_dram.rearrange("(j g) -> g j", g=P), base_i[:, :], allow_slow_non_contiguous=True).then_inc(base_out, 16)
                        sp.wait_ge(base_out, 16)
                        sp.dma_start(base_row[:, :], base_dram.rearrange("(o g) -> o g", o=1)).then_inc(base_in, 16)
                    before, slot = norm(it, c - 2, CU)
                    if exists(before):
                        store_z(before, slot)

            turn_b(0, U, base_step=True)
            with sp.Fori(1, TURNS) as it:
                turn_b(it, U)
            turn_b(TURNS, SHORT)
            n_tail = FULL // H % CU
            sp.wait_ge(e_turned, FULL - H)
            sp.dma_start(e_buf[0:TAIL_ROWS, 0, :], e_tail).then_inc(e_in[0], 16)
            for c in range(n_tail - 2, n_tail):
                store_z(TURNS, c)
            sp.wait_ge(z_saved, GROUPS)
            sp.dma_start(z_dram[CHUNKS, :, 0:TAIL_E], z_buf[:, 0, 0:TAIL_E]).then_inc(z_out[0], 16)
            sp.wait_ge(e_turned, GROUPS)
            for landed in z_out:
                sp.wait_ge(landed, 16 * U)

            def all_z_stored():
                sp.wait_ge(z_out[0], 16 * (CHUNKS // 2 + 1))
                sp.wait_ge(z_out[1], 16 * (CHUNKS // 2))

            def load_z(it, c):
                if isinstance(it, int) and it == 0 and c == 2:
                    all_z_stored()
                    sp.wait_ge(z_counted, GROUPS)
                wait(sp, elu_ready, (it - 1) * PU + -(-(c * H + H) // 2))
                sp.dma_start(zi_buf[:, c * H:(c + 1) * H, :].rearrange("p a b -> p (a b)"),
                             z_dram[ds(it * CU + c, 1), :, :].rearrange("n p f -> (n p) f")).then_inc(z_in[c], 16)

            def invert_counts():
                sp.dma_start(cnt_dram.rearrange("(o n) -> o n", o=1), agg[0:1, 1, 0:PARTS * COLS]).then_inc(cnt_out, 16)
                sp.wait_ge(cnt_out, 16)
                sp.dma_start(cnt_part, cnt_dram.rearrange("(p n) -> p n", p=PARTS)).then_inc(cnt_in, 16)
                sp.wait_ge(cnt_step, 3)
                sp.dma_start(inv_dram.rearrange("(p n) -> p n", p=PARTS), inv_part).then_inc(inv_out, 16)

            def take_inverse(n):
                sp.dma_start(agg[:, 1, ds(n * COLS, COLS)], inv_dram[ds(n * COLS, COLS)].partition_broadcast(P)).then_inc(inv_in, 16)

            def turn_c(it, groups):
                for c in range(groups // H):
                    load_z(it, c)
                    if not isinstance(it, int) and c == 0:
                        sp.wait_ge(inv_out, 16)
                        take_inverse(it - 1)
                if isinstance(it, int) and it == 0:
                    sp.wait_ge(cnt_added, GROUPS + 1)
                    invert_counts()

            sp.wait_ge(flag_ready, 1)
            wide = sp.value_load(flag[0:1, 0:1], min_val=0, max_val=N)
            with sp.If(wide < WIN):
                edge_turns(sp, turn_c)
                sp.wait_ge(elu_ready, (TURNS - 1) * PU + -(-(SHORT + 1) // 2))
                sp.dma_start(zi_buf[:, SHORT, 0:TAIL_E], z_dram[CHUNKS, :, 0:TAIL_E]).then_inc(z_in[SHORT // H], 16)
            with sp.Else():
                all_z_stored()
                sp.wait_ge(z_counted, GROUPS)
                with sp.Fori(0, CHUNKS) as n:
                    for s in range(H):
                        sp.wait_ge(slow_elu, n * H + s + 1)
                        sp.dma_start(e_buf[:, 0, :], z_dram[ds(n, 1), :, s * GE:(s + 1) * GE].rearrange("n p f -> (n p) f")).then_inc(slow_in, 16)
                sp.wait_ge(slow_elu, FULL + 1)
                sp.dma_start(e_buf[:, 0, 0:TAIL_E], z_dram[CHUNKS, :, 0:TAIL_E]).then_inc(slow_in, 16)
                sp.wait_ge(slow_added, GROUPS * NWIN + 1)
                invert_counts()
                sp.wait_ge(inv_out, 16)
                with sp.Fori(0, PARTS) as n:
                    take_inverse(n)

            def store_res(it, s):
                wait(sp, res_ready, it * U3 + s + 1)
                sp.dma_start(out_full[:, ds(it * U3 + s, 1), :, :].rearrange("p n t c -> p (n t) c"),
                             res_buf[:, s, :].rearrange("p (t c) -> p t c", c=C)).then_inc(res_out[s], 16)

            with sp.Fori(0, TURNS3) as it:
                for s in range(U3):
                    store_res(it, s)
            sp.wait_ge(res_ready, CHF + 1)
            sp.dma_start(out[CHF * CH:N, :], res_buf[0:CH_TAIL, 0, 0:C]).then_inc(res_out[0], 16)
            sp.wait_ge(res_out[0], 16 * (TURNS3 + 1))
            for s in range(1, U3):
                sp.wait_ge(res_out[s], 16 * TURNS3)

        @block.gpsimd
        def _(pool):
            pool.memset(src_raw[:, BLK - 1, :], 0).then_inc(idx_cleared, 1)
            pool.memset(dst_raw[:, BLK - 1, :], 0).then_inc(idx_cleared, 1)
            pool.memset(x_sb[:, NT - 1, :], 0.0).then_inc(x_cleared, 1)
            pool.memset(ident[:, :], 0.0).then_inc(ident_zero, 1)
            pool.memset(ones_bf[:, :], 1.0).then_inc(consts_ready, 1)
            for const, value in ((minus_half, -0.5), (minus_one, -1.0), (ln_eps, LN_EPS)):
                pool.memset(const[:, :], value).then_inc(consts_ready, 1)
            pool.iota(iota[:, :], [[1, SWIN]], base=0, channel_multiplier=0,
                      allow_small_or_imprecise_dtypes=True).then_inc(consts_ready, 1)
            pool.wait_ge(ident_zero, 1)
            pool.affine_select(out=ident[:, :], in_=ident[:, :], compare_op=ALU.not_equal, fill=1.0,
                               base=0, pattern=[[-1, P]], channel_multiplier=1).then_inc(consts_ready, 1)
            pool.wait_ge(consts_ready, 6)
            for i in range(LTURNS):
                tiles = slice(i * LT, (i + 1) * LT)
                pool.wait_ge(ln_step, (i + 1) * LT)
                pool.tensor_tensor(rstd[:, tiles], ln_mv[:, tiles, 1], ln_eps[:, :], ALU.add).then_inc(ln_root, 1)
                pool.wait_ge(ln_root, 3 * i + 1)
                pool.tensor_tensor(rstd[:, tiles], rstd[:, tiles], minus_half[:, :], ALU.pow).then_inc(ln_root, 1)
                pool.wait_ge(ln_root, 3 * i + 2)
                pool.tensor_tensor(ln_bias[:, tiles], ln_mv[:, tiles, 0], rstd[:, tiles], ALU.mult).then_inc(ln_root, 1)
                pool.wait_ge(ln_root, 3 * i + 3)
                pool.tensor_tensor(ln_bias[:, tiles], ln_bias[:, tiles], minus_one[:, :], ALU.mult).then_inc(ln_ready, 1)

            def take_indices(it, c, n):
                for s in range(c * H, c * H + H):
                    wait(pool, g_in[s], 16 * K * it)
                pool.tensor_copy(idx_now[:, c * H:c * H + n, :], src_idx[:, ds(count(it, c * H), n), :]).then_inc(idx_copied, 1)

            def gather(s, rows):
                for k in range(K):
                    pool.indirect_dma_start(
                        out=g_buf[0:rows, s, k * C:(k + 1) * C], out_offset=None,
                        in_=p_dram[:, :],
                        in_offset=bass.IndirectOffsetOnAxis(ap=idx_now[0:rows, s, k:k + 1].bitcast(U32), axis=0),
                    ).then_inc(g_in[s], 16)

            def turn_b(it, groups):
                for c in range(groups // H):
                    pool.wait_ge(idx_copied, it * CU + c + 1)
                    wait(pool, z_ready, count(it - 1, c * H + H))
                    if isinstance(it, int) and it == 0 and c == 1:
                        pool.wait_ge(idx_kept, BLK)
                    if isinstance(it, int) and it == TURNS and c == groups // H - 1:
                        take_indices(TURNS, c + 1, 1)
                    else:
                        take_indices(*norm(it, c + 1, CU), H)
                    for s in range(c * H, c * H + H):
                        gather(s, P)

            pool.wait_ge(idx_kept, 1)
            take_indices(0, 0, H)
            pool.wait_ge(p_out, 16 * LTURNS)
            edge_turns(pool, turn_b)
            pool.wait_ge(idx_copied, CHUNKS + 1)
            pool.wait_ge(z_ready, count(TURNS - 1, SHORT + 1))
            gather(SHORT, TAIL_ROWS)

            pool.wait_ge(bn_step, 1)
            pool.tensor_scalar(bn_k[:, 0:1], bn_mv[:, 1:2], BN_EPS, None, ALU.add).then_inc(bn_root, 1)
            pool.wait_ge(bn_root, 1)
            pool.tensor_tensor(bn_k[:, 0:1], bn_k[:, 0:1], minus_half[:, 0:1], ALU.pow).then_inc(bn_root, 1)

            def line(it, q, groups, cols):
                m = it * PU + q
                for c in sorted({2 * q // H, (2 * q + groups - 1) // H}):
                    pool.wait_ge(z_in[c], 16 * (it + 1))
                wait(pool, elu_turned, m - NPS + 1)

            def line_now(it, q, groups, cols):
                f = q % NPS * 2
                pool.tensor_scalar(f_buf[:, f:f + 2, :].rearrange("p a b -> p (a b)")[:, 0:cols],
                                   zi_buf[:, 2 * q:2 * q + 2, :].rearrange("p a b -> p (a b)")[:, 0:cols],
                                   bn_k[:, 1:2], bn_k[:, 4:5], ALU.mult, ALU.add).then_inc(lin_ready, 1)

            def add_window(it, s):
                n = count(it, s)
                base = pool.value_load(base_row[0:1, ds(n, 1)], min_val=0, max_val=N - 1)
                wait(pool, win_copied, it * PU + s // 2 + 1)
                wait(pool, win_added, n)
                table = agg[:, 0, ds(base, WIN)]
                pool.tensor_tensor(table, table, win_sum[:, s // 2 % 2, s % 2, :], ALU.add).then_inc(win_added, 1)

            LAG = 3
            def turn_c(it, groups):
                for q in range(groups // 2):
                    after, slot = norm(it, q + 2, PU)
                    following = (after, slot, 2, 2 * GE)
                    if isinstance(it, int) and it == TURNS and slot == SHORT // 2:
                        following = (TURNS, slot, 1, TAIL_E)
                    ends = isinstance(it, int) and it == TURNS and slot > SHORT // 2
                    if not ends:
                        line(*following)
                    before, slot = norm(it, 2 * q - 2 * LAG, U)
                    if exists(before):
                        add_window(before, slot)
                    if not ends:
                        line_now(*following)
                    if exists(before):
                        add_window(before, slot + 1)

            pool.wait_ge(flag_ready, 1)
            pool.wait_ge(base_in, 16)
            pool.wait_ge(bn1_ready, 1)
            wide = pool.value_load(flag[0:1, 0:1], min_val=0, max_val=N)
            with pool.If(wide < WIN):
                pool.wait_ge(z_ready, GROUPS)
                for q in range(2):
                    line(0, q, 2, 2 * GE)
                    line_now(0, q, 2, 2 * GE)
                edge_turns(pool, turn_c)
                for s in range(SHORT - 2 * LAG, SHORT + 1):
                    add_window(*norm(TURNS, s, U))
                pool.wait_ge(win_added, GROUPS)
            with pool.Else():
                pool.wait_ge(slow_added, GROUPS * NWIN + 1)

            pool.wait_ge(inv_in, 16 * PARTS)
            def ratio(it, s, cols):
                n = it * U3 + s
                cs = ds(n * CH, cols)
                wait(pool, mean_ready, n - U3 + 1)
                pool.tensor_tensor(ratio_buf[:, s, 0:cols], agg[:, 0, cs], agg[:, 1, cs], ALU.mult).then_inc(ratio_ready, 1)

            node_chunks(pool, ratio)
            pool.wait_ge(bn_step, 6)
            pool.tensor_scalar(bn2_k[:, 0:1], bn2_mv[:, 1:2], BN_EPS, None, ALU.add).then_inc(bn_root, 1)
            pool.wait_ge(bn_root, 3)
            pool.tensor_tensor(bn2_k[:, 0:1], bn2_k[:, 0:1], minus_half[:, 0:1], ALU.pow).then_inc(bn_root, 1)

        @block.tensor
        def _(pe):
            pe.wait_ge(consts_ready, 6)
            pe.wait_ge(w_in, 32)
            for i, w in enumerate((w1_sb, w2_sb)):
                for j in range(2):
                    last = pe.transpose(ps[:, 6, (2 * i + j) * C:(2 * i + j + 1) * C], w[:, j * C:(j + 1) * C], ident[:, :])
            last.then_inc(w_turned, 1)

            def turn_indices(what, ready, value, first):
                pe.wait_ge(ready, value)
                for n in range(first, first + BLK):
                    if n >= 2:
                        pe.wait_ge(idx_kept, n - 1)
                    for k in range(K):
                        last = pe.transpose(ps[:, 7 - n % 2, k * P:(k + 1) * P], what[:, n - first, k:GE:K], ident[:, :])
                    last.then_inc(idx_turned, 1)

            tr_bank = ps[:, 0:2, :].rearrange("p a b -> p (a b)")
            p_bank = ps[:, 2:4, :].rearrange("p a b -> p (a b)")
            pe.wait_ge(wT_ready, 2)
            def turn_a(it):
                wait(pe, hT_copied, it)
                for t in range(LT):
                    pe.wait_ge(h_ready, it * LT + t + 1)
                    last = pe.transpose(tr_bank[:, t * P:(t + 1) * P], h_st[:, t * P:(t + 1) * P], ident[:, :])
                last.then_inc(h_turned, 1)
                pe.wait_ge(hT_copied, it + 1)
                wait(pe, p_added, it)
                for t in range(LT):
                    last = pe.matmul(p_bank[:, t * P:(t + 1) * P], hT_st[:, t * P:(t + 1) * P], wT[:, 0, :], start=True, stop=True)
                last.then_inc(p_product, 1)
            node_turns(pe, turn_a)
            turn_indices(src_f, idx_float, 1, 0)
            turn_indices(rel_f, rel_ready, BLK, BLK)
            turn_indices(dst_f, rel_ready, BLK, 2 * BLK)
            pe.wait_ge(span_step, 2)
            pe.wait_ge(idx_kept, 3 * BLK)
            pe.transpose(ps[0:1, 6, 0:P], dspan1[:, 0:1], ident[:, :]).then_inc(span_turned, 1)
            pe.wait_ge(p_added, LTURNS)
            pe.wait_ge(flag_ready, 1)

            def turn_edges(it, s, rows):
                n = count(it, s)
                if s % H == 0:
                    pe.wait_ge(e_in[s // H % 2], 16 * (uses(it, s, EB) + 1))
                wait(pe, eT_ready, n - NPS + 1)
                for k in range(K):
                    last = pe.transpose(edge_bank[s % NPS][:, k * rows:(k + 1) * rows],
                                        e_buf[0:rows, s % EB, k * C:(k + 1) * C], ident[0:rows, 0:rows])
                last.then_inc(e_turned, 1)

            def product(it, s, rows):
                n = count(it, s)
                bank = z_bank[s % NPS]
                pe.wait_ge(eT_ready, n + 1)
                wait(pe, z_saved, n - NPS + 1)
                pe.matmul(bank[:, 0:K * rows], wT[:, 1, :], t_buf[:, s % NPS, 0:K * rows], start=True, stop=False)
                pe.wait_ge(g_in[s], 16 * K * (it + 1))
                for k in range(K):
                    last = pe.matmul(bank[:, k * rows:(k + 1) * rows], g_buf[0:rows, s, k * C:(k + 1) * C],
                                     ident[0:rows, 0:rows], start=False, stop=(k == K - 1))
                last.then_inc(z_ready, 1)

            def window_counts(it, s, rows):
                n = count(it, s)
                pe.wait_ge(cnt_hot, n + 1)
                wait(pe, cnt_added, n)
                for k in range(K):
                    last = pe.matmul(win_bank[s % 2][:, 0:WIN], ones_bf[0:rows, :], hot_bf[0:rows, s % NPS, k, :],
                                     start=(k == 0), stop=(k == K - 1))
                last.then_inc(cnt_ready, 1)

            def turn_b(it, groups):
                for s in range(groups):
                    if isinstance(it, int) and it == TURNS and s == groups - 1:
                        turn_edges(*TAIL, TAIL_ROWS)
                    else:
                        turn_edges(*norm(it, s + 1, U), P)
                    window_counts(it, s, P)
                    product(it, s, P)

            turn_edges(0, 0, P)
            edge_turns(pe, turn_b)
            window_counts(*TAIL, TAIL_ROWS)
            product(*TAIL, TAIL_ROWS)
            pe.wait_ge(z_saved, GROUPS)
            pe.wait_ge(cnt_added, GROUPS + 1)

            pair_bank = [ps[:, 2 * b:2 * b + 2, :] for b in range(2)]

            def turn_elu(it, q, groups, rows):
                m = it * PU + q
                f = q % NPS * 2
                pe.wait_ge(elu_ready, m + 1)
                wait(pe, elu_edges, m - 2 + 1)
                for g in range(groups):
                    for k in range(K):
                        last = pe.transpose(pair_bank[q % 2][0:rows, g, k * C:(k + 1) * C],
                                            f_buf[:, f + g, k * rows:(k + 1) * rows], ident[:, :])
                last.then_inc(elu_turned, 1)

            def windows(it, q, groups, rows):
                m = it * PU + q
                pe.wait_ge(elu_edges, m + 1)
                pe.wait_ge(hot_ready, m + 1)
                wait(pe, rows_copied, m - 2 + 1)
                for k in range(K):
                    for g in range(groups):
                        last = pe.matmul(ps[g * HALF:(g + 1) * HALF, 4 + q % 2, 0:C], one_hot[0:rows, q % NPS, g, k, :],
                                         m_buf[0:rows, q % NPS * 2 + g, k * C:(k + 1) * C],
                                         start=(k == 0), stop=(k == K - 1), tile_position=(0, g * HALF))
                last.then_inc(win_ready, 1)

            def turn_windows(it, q, groups):
                m = it * PU + q
                used = groups * HALF
                pe.wait_ge(rows_copied, m + 1)
                wait(pe, win_copied, m - 2 + 1)
                pe.transpose(ps[:, 6 + q % 2, 0:used], win_rows[0:used, q % 2, :], ident[0:used, 0:used]).then_inc(win_turned, 1)

            def turn_c(it, groups):
                for q in range(groups // 2):
                    turn_elu(it, q, 2, P)
                    before, slot = norm(it, q - 2, PU)
                    if exists(before):
                        turn_windows(before, slot, 2)
                    before, slot = norm(it, q - 1, PU)
                    if exists(before):
                        windows(before, slot, 2, P)

            pe.wait_ge(flag_ready, 1)
            wide = pe.value_load(flag[0:1, 0:1], min_val=0, max_val=N)
            with pe.If(wide < WIN):
                edge_turns(pe, turn_c)
                turn_elu(TURNS, SHORT // 2, 1, TAIL_ROWS)
                turn_windows(TURNS, SHORT // 2 - 2, 2)
                windows(TURNS, SHORT // 2 - 1, 2, P)
                windows(TURNS, SHORT // 2, 1, TAIL_ROWS)
                turn_windows(TURNS, SHORT // 2 - 1, 2)
                turn_windows(TURNS, SHORT // 2, 1)
            with pe.Else():
                def slow_group(n, rows):
                    pe.wait_ge(slow_elu, n + 2)
                    for k in range(K):
                        last = pe.transpose(edge_bank[0][0:rows, k * C:(k + 1) * C],
                                            z_buf[:, 0, k * rows:(k + 1) * rows], ident[:, :])
                    last.then_inc(slow_turned, 1)
                    with pe.Fori(0, NWIN) as w:
                        pe.wait_ge(slow_edges, n + 1)
                        step = n * NWIN + w
                        pe.wait_ge(slow_hot, step + 1)
                        pe.wait_ge(slow_added, step + 1)
                        hot = z_buf[0:rows, 2:2 + K, :]
                        for k in range(K):
                            pe.matmul(win_bank[0][:, :], g_buf[0:rows, 0, k * C:(k + 1) * C], hot[:, k, :],
                                      start=(k == 0), stop=(k == K - 1))
                        for k in range(K):
                            last = pe.matmul(win_bank[1][:, :], ones_bf[0:rows, :], hot[:, k, :].bitcast(BF16)[:, 1:2 * SWIN:2],
                                             start=(k == 0), stop=(k == K - 1))
                        last.then_inc(slow_win, 1)
                with pe.Fori(0, FULL) as n:
                    slow_group(n, P)
                slow_group(FULL, TAIL_ROWS)

            def node_product(it, s, cols):
                n = it * U3 + s
                pe.wait_ge(mean_ready, n + 1)
                wait(pe, y_kept, n - U3 + 1)
                cs = ds(n * CH, cols)
                pe.matmul(y_bank[s][:, 0:cols], wT[:, 2, :], hT[:, cs], start=True, stop=False)
                pe.matmul(y_bank[s][:, 0:cols], wT[:, 3, :], t_buf[:, s, 0:cols], start=False, stop=True).then_inc(y_ready, 1)

            def turn_nodes(it, s, cols):
                n = it * U3 + s
                pe.wait_ge(yelu_ready, n + 1)
                wait(pe, res_ready, n - U3 + 1)
                for t in range(-(-cols // P)):
                    rows = min(P, cols - t * P)
                    last = pe.transpose(turn_bank[s][0:rows, t * C:(t + 1) * C], node_buf[:, s, t * P:t * P + rows], ident[:, :])
                last.then_inc(yelu_turned, 1)

            node_chunks(pe, node_product)
            node_chunks(pe, turn_nodes)

        @block.scalar
        def _(act):
            act.dma_start(w1_sb[:, :], w1).then_inc(w_in, 16)
            act.dma_start(w2_sb[:, :], w2).then_inc(w_in, 16)
            act.dma_start(b1_rows[:, :], b1.partition_broadcast(P)).then_inc(vec_in, 16)

            def keep_indices(kept, first):
                for n in range(first, first + BLK):
                    j = n - first
                    act.wait_ge(idx_turned, n + 1)
                    size = min(P, GROUPS - j * P)
                    act.activation(kept[:, j * P:j * P + size, :].rearrange("p g k -> p k g"),
                                   ps[:, 7 - n % 2, :].rearrange("p (k g) -> p k g", k=K)[:, :, 0:size], ACT.Copy).then_inc(idx_kept, 1)

            tr_bank = ps[:, 0:2, :].rearrange("p a b -> p (a b)")
            def rectify(it):
                act.wait_ge(ln_ready, it + 1)
                wait(act, h_turned, it)
                for t in range(LT):
                    act.activation(h_st[:, t * P:(t + 1) * P], x_sb[:, ds(it * LT + t, 1), :].rearrange("p n c -> p (n c)"),
                                   ACT.Relu, bias=ln_bias[:, ds(it * LT + t, 1)], scale=rstd[:, ds(it * LT + t, 1)]).then_inc(h_ready, 1)

            def copy_hT(it):
                act.wait_ge(h_turned, it + 1)
                wait(act, p_product, it)
                wait(act, hT_saved, it)
                act.activation(hT_st, tr_bank[:, 0:LT * P], ACT.Copy).then_inc(hT_copied, 1)

            def turn_a(it):
                rectify(it)
                copy_hT(it)

            node_turns(act, turn_a)
            keep_indices(src_idx, 0)
            keep_indices(rel_dst, BLK)
            keep_indices(abs_dst, 2 * BLK)

            def keep_eT(it, s, rows):
                n = count(it, s)
                act.wait_ge(e_turned, n + 1)
                wait(act, z_ready, n - NPS + 1)
                act.activation(t_buf[:, s % NPS, 0:K * rows], edge_bank[s % NPS][:, 0:K * rows], ACT.Copy).then_inc(eT_ready, 1)

            def keep_z(it, s, rows):
                n = count(it, s)
                act.wait_ge(z_ready, n + 1)
                if s % H == 0:
                    wait(act, z_out[s // H % 2], 16 * uses(it, s, EB))
                wait(act, z_counted, n - EB + 1)
                act.activation(z_buf[:, s % EB, 0:K * rows], z_bank[s % NPS][:, 0:K * rows], ACT.Copy).then_inc(z_saved, 1)

            def turn_b(it, groups):
                for s in range(groups):
                    keep_eT(it, s, P)
                    before, slot = norm(it, s - 1, U)
                    if exists(before):
                        keep_z(before, slot, P)

            edge_turns(act, turn_b)
            keep_eT(*TAIL, TAIL_ROWS)
            keep_z(TURNS, SHORT - 1, P)
            keep_z(*TAIL, TAIL_ROWS)

            def exponent(it, q, groups, cols):
                m = it * PU + q
                for c in sorted({2 * q // H, (2 * q + groups - 1) // H}):
                    act.wait_ge(z_in[c], 16 * (it + 1))
                wait(act, elu_ready, m - NPS + 1)
                act.activation(x_buf[q % NPS][:, 0:cols],
                               zi_buf[:, 2 * q:2 * q + 2, :].rearrange("p a b -> p (a b)")[:, 0:cols], ACT.Exp,
                               bias=bn_k[:, 3:4], scale=bn_k[:, 1:2]).then_inc(exp_ready, 1)

            def keep_elu(it, q, groups, rows):
                m = it * PU + q
                act.wait_ge(elu_turned, m + 1)
                wait(act, win_ready, m - NPS + 1)
                f = q % NPS * 2
                b = q % 2 * 2
                act.activation(m_buf[0:rows, f:f + groups, :], ps[0:rows, b:b + groups, :], ACT.Copy).then_inc(elu_edges, 1)

            def turn_c(it, groups):
                for q in range(groups // 2):
                    if isinstance(it, int) and it == TURNS and q == SHORT // 2 - 1:
                        exponent(TURNS, SHORT // 2, 1, TAIL_E)
                    else:
                        exponent(*norm(it, q + 1, PU), 2, 2 * GE)
                    before, slot = norm(it, q - 1, PU)
                    if exists(before):
                        keep_elu(before, slot, 2, P)

            act.wait_ge(flag_ready, 1)
            wide = act.value_load(flag[0:1, 0:1], min_val=0, max_val=N)
            act.wait_ge(bn1_ready, 1)
            with act.If(wide < WIN):
                act.wait_ge(z_ready, GROUPS)
                exponent(0, 0, 2, 2 * GE)
                edge_turns(act, turn_c)
                keep_elu(TURNS, SHORT // 2 - 1, 2, P)
                keep_elu(TURNS, SHORT // 2, 1, TAIL_ROWS)
            with act.Else():
                def slow_group(n, rows):
                    act.wait_ge(slow_in, 16 * (n + 1))
                    act.activation(t_buf[:, 0, 0:K * rows], e_buf[:, 0, 0:K * rows], ACT.Exp,
                                   bias=bn_k[:, 3:4], scale=bn_k[:, 1:2]).then_inc(slow_exp, 1)
                    act.wait_ge(slow_turned, n + 2)
                    act.wait_ge(slow_win, n * NWIN + 1)
                    act.activation(g_buf[0:rows, 0, :], edge_bank[0][0:rows, :], ACT.Copy).then_inc(slow_edges, 1)
                with act.Fori(0, FULL) as n:
                    slow_group(n, P)
                slow_group(FULL, TAIL_ROWS)

            def keep_y(it, s, cols):
                n = it * U3 + s
                act.wait_ge(y_ready, n + 1)
                act.activation(hT[:, ds(n * CH, cols)], y_bank[s][:, 0:cols], ACT.Identity, bias=vecs[:, 2:3]).then_inc(y_kept, 1)

            def node_exponent(it, s, cols):
                n = it * U3 + s
                wait(act, yelu_turned, n - U3 + 1)
                act.activation(t_buf[:, s, 0:cols], hT[:, ds(n * CH, cols)], ACT.Exp,
                               bias=bn2_k[:, 3:4], scale=bn2_k[:, 1:2]).then_inc(yexp_ready, 1)
                act.activation(node_buf[:, s, 0:cols], hT[:, ds(n * CH, cols)], ACT.Identity,
                               bias=bn2_k[:, 4:5], scale=bn2_k[:, 1:2]).then_inc(ylin_ready, 1)

            node_chunks(act, keep_y)
            act.wait_ge(bn2_ready, 1)
            node_chunks(act, node_exponent)

        @block.vector
        def _(dve):
            p_bank = ps[:, 2:4, :].rearrange("p a b -> p (a b)")
            def layer_statistics(it):
                for t in range(it * LT, it * LT + LT):
                    dve.bn_stats(ln_st[:, t, :], x_sb[:, t, :])
                dve.drain()
                for t in range(it * LT, it * LT + LT):
                    dve.bn_aggr(ln_mv[:, t, :], ln_st[:, t, :]).then_inc(ln_step, 1)

            def node_table(it):
                dve.wait_ge(hT_copied, it + 1)
                dve.tensor_copy(hT[:, ds(it * LT * P, LT * P)], hT_st).then_inc(hT_saved, 1)
                dve.wait_ge(p_product, it + 1)
                wait(dve, p_out, 16 * it)
                dve.tensor_tensor(p_st.rearrange("p (t c) -> p t c", c=C), p_bank[:, 0:LT * P].rearrange("p (t c) -> p t c", c=C),
                                  b1_rows[:, :].unsqueeze(1).to_broadcast([P, LT, C]), ALU.add).then_inc(p_added, 1)

            dve.wait_ge(x_first, 16)
            layer_statistics(0)
            dve.wait_ge(w_turned, 1)
            dve.tensor_copy(wT[:, 0:3, :].rearrange("p a b -> p (a b)"), ps[:, 6, 0:3 * C]).then_inc(wT_ready, 1)
            dve.tensor_scalar(wT[:, 3, :], ps[:, 6, 3 * C:4 * C], -1.0, None, ALU.mult).then_inc(wT_ready, 1)
            AHEAD = 3
            dve.wait_ge(x_second, 16)
            for it in range(1, AHEAD):
                layer_statistics(it)
            dve.wait_ge(x_in, 32)
            layer_statistics(AHEAD)
            dve.wait_ge(vec_in, 16 * 6)
            for it in range(LTURNS):
                node_table(it)
                if it + 1 + AHEAD < LTURNS:
                    layer_statistics(it + 1 + AHEAD)
                if it == AHEAD:
                    dve.wait_ge(src_in, 64)
                    dve.tensor_copy(src_f, src_raw).then_inc(idx_float, 1)
            dve.wait_ge(dst_in, 64)
            dve.tensor_copy(dst_f, dst_raw).then_inc(idx_float, 1)
            dve.wait_ge(idx_float, 2)
            dve.tensor_reduce(dmin[:, :], dst_f, AX_X, ALU.min).then_inc(dminmax, 1)
            dve.tensor_reduce(dmax[:, :], dst_f, AX_X, ALU.max).then_inc(dminmax, 1)
            dve.wait_ge(dminmax, 2)
            for j in range(BLK):
                dve.tensor_scalar(rel_f[:, j, :], dst_f[:, j, :], dmin[:, j:j + 1], None, ALU.subtract).then_inc(rel_ready, 1)
            dve.tensor_copy(base_i[:, :], dmin[:, :]).then_inc(base_ready, 1)
            dve.tensor_tensor(dspan[:, :], dmax[:, :], dmin[:, :], ALU.subtract).then_inc(span_step, 1)
            dve.wait_ge(span_step, 1)
            dve.tensor_reduce(dspan1[:, :], dspan[:, :], AX_X, ALU.max).then_inc(span_step, 1)
            dve.wait_ge(span_turned, 1)
            dve.tensor_reduce(span_all[:, :], ps[0:1, 6, 0:P], AX_X, ALU.max).then_inc(span_step, 1)
            dve.wait_ge(span_step, 3)
            dve.tensor_copy(flag[:, :], span_all[:, :]).then_inc(flag_ready, 1)

            dve.wait_ge(idx_kept, 3 * BLK)
            dve.memset(agg_flat, 0.0).then_inc(cnt_added, 1)
            dve.memset(one_hot[:, :, :, :, :].rearrange("p n g k w -> p (n g k w)"), 0.0).then_inc(hot_cleared, 1)
            dve.wait_ge(hot_cleared, 1)
            dve.wait_ge(base_in, 16)

            def statistics(it, s, rows):
                n = count(it, s)
                dve.wait_ge(z_saved, n + 1)
                dve.bn_stats(stats[:, ds(n, 1), :].rearrange("p n f -> p (n f)"), z_buf[:, s % EB, 0:K * rows]).then_inc(z_counted, 1)

            def hot(matrix, n, groups, rows):
                return dve.tensor_tensor(
                    matrix,
                    rel_dst[0:rows, ds(n, groups), :].rearrange("p n k -> p (n k)").unsqueeze(2).to_broadcast([rows, groups * K, WIN]),
                    iota[0:rows, 0:WIN].unsqueeze(1).to_broadcast([rows, groups * K, WIN]),
                    ALU.is_equal)

            def count_hot(it, s, rows):
                n = count(it, s)
                wait(dve, cnt_ready, n - NPS + 1)
                hot(hot_bf[0:rows, s % NPS, :, :], n, 1, rows).then_inc(cnt_hot, 1)

            def add_counts(it, s):
                n = count(it, s)
                base = dve.value_load(base_row[0:1, ds(n, 1)], min_val=0, max_val=N - 1)
                dve.wait_ge(cnt_ready, n + 1)
                dve.wait_ge(cnt_added, n + 1)
                table = agg[:, 1, ds(base, WIN)]
                dve.tensor_tensor(table, table, win_bank[s % 2][:, 0:WIN], ALU.add).then_inc(cnt_added, 1)

            def turn_b(it, groups):
                for s in range(groups):
                    count_hot(it, s, P)
                    before, slot = norm(it, s - 1, U)
                    if exists(before):
                        add_counts(before, slot)
                        statistics(before, slot, P)

            edge_turns(dve, turn_b)
            count_hot(*TAIL, TAIL_ROWS)
            add_counts(TURNS, SHORT - 1)
            statistics(TURNS, SHORT - 1, P)
            add_counts(*TAIL)
            statistics(*TAIL, TAIL_ROWS)

            def bn_constants(mv, k, weight, bias, first, root):
                dve.wait_ge(bn_root, root)
                dve.tensor_tensor(k[:, 1:2], k[:, 0:1], weight, ALU.mult).then_inc(bn_step, 1)
                dve.wait_ge(bn_step, first + 1)
                dve.tensor_tensor(k[:, 2:3], mv[:, 0:1], k[:, 1:2], ALU.mult).then_inc(bn_step, 1)
                dve.wait_ge(bn_step, first + 2)
                dve.tensor_tensor(k[:, 3:4], bias, k[:, 2:3], ALU.subtract).then_inc(bn_step, 1)
                dve.wait_ge(bn_step, first + 3)
                dve.tensor_scalar(k[:, 4:5], k[:, 3:4], 1.0, None, ALU.add).then_inc(bn_step, 1)
                dve.wait_ge(bn_step, first + 4)

            dve.wait_ge(z_counted, GROUPS)
            dve.bn_aggr(bn_mv[:, :], stats[:, :, :].rearrange("p n f -> p (n f)")).then_inc(bn_step, 1)
            bn_constants(bn_mv, bn_k, vecs[:, 0:1], vecs[:, 1:2], 1, 2)
            dve.engine_nop().then_inc(bn1_ready, 1)

            def elu(it, q, cols):
                m = it * PU + q
                f = q % NPS * 2
                line = f_buf[:, f:f + 2, :].rearrange("p a b -> p (a b)")[:, 0:cols]
                dve.wait_ge(lin_ready, m + 1)
                dve.wait_ge(exp_ready, m + 1)
                dve.scalar_tensor_tensor(out=line, in0=x_buf[q % NPS][:, 0:cols],
                                         scalar=1.0, in1=line, op0=ALU.min, op1=ALU.max).then_inc(elu_ready, 1)

            def sum_hot(it, q, groups, rows):
                m = it * PU + q
                wait(dve, win_ready, m - NPS + 1)
                hot(one_hot[0:rows, q % NPS, 0:groups, :, 0:WIN].rearrange("p g k w -> p (g k) w"),
                    count(it, 2 * q), groups, rows).then_inc(hot_ready, 1)

            def copy_rows(it, q, groups):
                m = it * PU + q
                used = groups * HALF
                dve.wait_ge(win_ready, m + 1)
                wait(dve, win_turned, m - 2 + 1)
                dve.tensor_copy(win_rows[0:used, q % 2, :], ps[0:used, 4 + q % 2, 0:C]).then_inc(rows_copied, 1)

            def copy_windows(it, q, groups):
                m = it * PU + q
                dve.wait_ge(win_turned, m + 1)
                wait(dve, win_added, 2 * (m - 1))
                dve.tensor_copy(win_sum[:, q % 2, 0:groups, :],
                                ps[:, 6 + q % 2, 0:groups * HALF].rearrange("p (g w) -> p g w", w=HALF)[:, :, 0:WIN]).then_inc(win_copied, 1)

            def invert_counts():
                dve.wait_ge(cnt_in, 16)
                dve.tensor_scalar(inv_part, cnt_part, 1.0, None, ALU.max).then_inc(cnt_step, 1)
                dve.wait_ge(cnt_step, 1)
                dve.reciprocal(inv_part, inv_part).then_inc(cnt_step, 1)
                dve.wait_ge(cnt_step, 2)
                dve.scalar_tensor_tensor(out=inv_part, in0=cnt_part, scalar=1.0, in1=inv_part, op0=ALU.min, op1=ALU.mult).then_inc(cnt_step, 1)

            def turn_c(it, groups):
                for q in range(groups // 2):
                    elu(it, q, 2 * GE)
                    if isinstance(it, int) and it == 0 and q == 2:
                        invert_counts()
                    sum_hot(it, q, 2, P)
                    before, slot = norm(it, q - 2, PU)
                    if exists(before):
                        copy_rows(before, slot, 2)
                    before, slot = norm(it, q - 3, PU)
                    if exists(before):
                        copy_windows(before, slot, 2)

            wide = dve.value_load(flag[0:1, 0:1], min_val=0, max_val=N)
            with dve.If(wide < WIN):
                edge_turns(dve, turn_c)
                elu(TURNS, SHORT // 2, TAIL_E)
                sum_hot(TURNS, SHORT // 2, 1, TAIL_ROWS)
                copy_rows(TURNS, SHORT // 2 - 2, 2)
                copy_windows(TURNS, SHORT // 2 - 3, 2)
                copy_rows(TURNS, SHORT // 2 - 1, 2)
                copy_windows(TURNS, SHORT // 2 - 2, 2)
                copy_rows(TURNS, SHORT // 2, 1)
                copy_windows(TURNS, SHORT // 2 - 1, 2)
                copy_windows(TURNS, SHORT // 2, 1)
            with dve.Else():
                for ahead in (slow_elu, slow_turned, slow_win):
                    dve.engine_nop().then_inc(ahead, 1)
                dve.wait_ge(cnt_added, GROUPS + 1)
                dve.memset(agg[:, 1, :], 0.0).then_inc(slow_added, 1)
                dve.wait_ge(slow_added, 1)

                def slow_group(n, rows):
                    line = z_buf[:, 0, 0:K * rows]
                    now = one_hot[:, 0, 0, 0, 0:K]
                    dve.wait_ge(slow_in, 16 * (n + 1))
                    dve.wait_ge(slow_turned, n + 1)
                    dve.tensor_scalar(line, e_buf[:, 0, 0:K * rows], bn_k[:, 1:2], bn_k[:, 4:5], ALU.mult, ALU.add).then_inc(slow_lin, 1)
                    dve.wait_ge(slow_lin, n + 1)
                    dve.wait_ge(slow_exp, n + 1)
                    dve.scalar_tensor_tensor(out=line, in0=t_buf[:, 0, 0:K * rows], scalar=1.0, in1=line,
                                             op0=ALU.min, op1=ALU.max).then_inc(slow_elu, 1)
                    dve.tensor_copy(now, abs_dst[:, ds(n, 1), :].rearrange("p n k -> p (n k)")).then_inc(slow_dst, 1)
                    with dve.Fori(0, NWIN) as w:
                        step = n * NWIN + w
                        dve.wait_ge(slow_dst, n * (NWIN + 1) + w + 1)
                        dve.wait_ge(slow_win, step + 1)
                        for k in range(K):
                            last = dve.tensor_scalar(z_buf[:, 2 + k, :], iota[:, :], now[:, k:k + 1], None, ALU.is_equal)
                        last.then_inc(slow_hot, 1)
                        dve.wait_ge(slow_hot, step + 1)
                        dve.tensor_scalar(now, now, float(SWIN), None, ALU.subtract).then_inc(slow_dst, 1)
                        dve.wait_ge(slow_win, step + 2)
                        table = agg[:, :, ds(w * SWIN, SWIN)]
                        dve.tensor_tensor(table, table, ps[:, 6:8, :], ALU.add).then_inc(slow_added, 1)
                        dve.wait_ge(slow_added, step + 2)
                with dve.Fori(0, FULL) as n:
                    slow_group(n, P)
                slow_group(FULL, TAIL_ROWS)
                invert_counts()

            def mean(it, s, cols):
                n = it * U3 + s
                dve.wait_ge(ratio_ready, n + 1)
                wait(dve, y_ready, n - U3 + 1)
                dve.scalar_tensor_tensor(out=t_buf[:, s, 0:cols], in0=agg[:, 1, ds(n * CH, cols)], scalar=0.0,
                                         in1=ratio_buf[:, s, 0:cols], op0=ALU.is_gt, op1=ALU.subtract).then_inc(mean_ready, 1)

            def node_statistics(it, s, cols):
                n = it * U3 + s
                dve.wait_ge(y_kept, n + 1)
                dve.bn_stats(stats2[:, ds(n, 1), :].rearrange("p n f -> p (n f)"), hT[:, ds(n * CH, cols)]).then_inc(y_counted, 1)

            def node_elu(it, s, cols):
                n = it * U3 + s
                line = node_buf[:, s, 0:cols]
                dve.wait_ge(ylin_ready, n + 1)
                dve.wait_ge(yexp_ready, n + 1)
                dve.scalar_tensor_tensor(out=line, in0=t_buf[:, s, 0:cols], scalar=1.0, in1=line,
                                         op0=ALU.min, op1=ALU.max).then_inc(yelu_ready, 1)

            def residual(it, s, cols):
                n = it * U3 + s
                tiles = -(-cols // P)
                rows = min(P, cols)
                dve.wait_ge(yelu_turned, n + 1)
                wait(dve, res_out[s], 16 * it)
                dve.scalar_tensor_tensor(out=res_buf[0:rows, s, 0:tiles * C], in0=turn_bank[s][0:rows, 0:tiles * C], scalar=-1.0,
                                         in1=x_sb[0:rows, ds(n * (CH // P), tiles), :].rearrange("p t c -> p (t c)"),
                                         op0=ALU.add, op1=ALU.add).then_inc(res_ready, 1)

            LAG = 2
            for first, second in ((mean, node_statistics), (node_elu, residual)):
                def turn_nodes(it, chunks, cols):
                    for s in range(chunks):
                        first(it, s, cols)
                        before, slot = norm(it, s - LAG, U3)
                        if exists(before):
                            second(before, slot, CH)
                turn_nodes(0, U3, CH)
                with dve.Fori(1, TURNS3) as it:
                    turn_nodes(it, U3, CH)
                turn_nodes(TURNS3, 1, CH_TAIL)
                second(TURNS3 - 1, U3 - 1, CH)
                second(TURNS3, 0, CH_TAIL)
                if first is mean:
                    dve.wait_ge(y_counted, CHF + 1)
                    dve.bn_aggr(bn2_mv[:, :], stats2[:, :, :].rearrange("p n f -> p (n f)")).then_inc(bn_step, 1)
                    bn_constants(bn2_mv, bn2_k, vecs[:, 3:4], vecs[:, 4:5], 6, 4)
                    dve.engine_nop().then_inc(bn2_ready, 1)


_INS = ["x", "src", "dst", "edge_attr_128", "L0_gnn_w1", "L0_gnn_b1", "L0_gnn_bn1_w", "L0_gnn_bn1_b",
        "L0_gnn_w2", "L0_gnn_b2", "L0_gnn_bn2_w", "L0_gnn_bn2_b"]


def kernel(**inputs):
    import numpy as _np
    import concourse.bacc as _bacc
    from concourse import mybir as _mybir
    from concourse.bass_utils import run_bass_kernel_spmd as _run

    nc = _bacc.Bacc("TRN2", target_bir_lowering=False, num_devices=1)
    arrays, args = {}, []
    for name in _INS:
        a = _np.ascontiguousarray(inputs[name])
        arrays[f"in_{name}"] = a
        args.append(nc.dram_tensor(f"in_{name}", a.shape, _mybir.dt.from_np(a.dtype), kind="ExternalInput").ap())
    shape = inputs["x"].shape
    args.append(nc.dram_tensor("out_0", shape, _mybir.dt.float32, kind="ExternalOutput").ap())
    gnn_kernel(nc, *args)
    r = _run(nc, [arrays], core_ids=[0])
    return r.results[0]["out_0"]
```
